# Optimizing a Trainium2 kernel written in Bass

```python
import numpy as np
import jax
import jax.numpy as jnp

def _softmax(x, axis=-1):
    return jax.nn.softmax(x, axis=axis)

def _gelu(x):
    return jax.nn.gelu(x, approximate=True)

def _silu(x):
    return jax.nn.silu(x)

def _sigmoid(x):
    return jax.nn.sigmoid(x)

def _layernorm(x, axis=-1, eps=1e-05):
    m = jnp.mean(x, axis=axis, keepdims=True)
    v = jnp.var(x, axis=axis, keepdims=True)
    return (x - m) / jnp.sqrt(v + eps)

def _scatter_add(tgt, idx, src, axis=0):
    return tgt.at[idx].add(src)

def _segment_sum(src, seg, n):
    return jax.ops.segment_sum(src, seg, n)
kernel_name = 'mk_adaln_d1_jaxref_r8_2fb051'

def setup_inputs(seed: int=0):
    np.random.seed(seed)
    _w = jnp.asarray

    def _L0_attn_setup():
        import jax, jax.numpy as jnp
        import numpy as np
        HIDDEN = 128
        HEADS = 16
        HEAD_DIM = HIDDEN // HEADS
        key = jax.random.key(seed)
        ks = jax.random.split(key, 9)
        s = 1.0 / np.sqrt(HIDDEN)
        x = jax.random.normal(ks[0], (2, 256, HIDDEN), dtype=jnp.float32)
        Wq = jax.random.uniform(ks[1], (HIDDEN, HIDDEN), jnp.float32, -s, s)
        bq = jax.random.uniform(ks[2], (HIDDEN,), jnp.float32, -s, s)
        Wk = jax.random.uniform(ks[3], (HIDDEN, HIDDEN), jnp.float32, -s, s)
        bk = jax.random.uniform(ks[4], (HIDDEN,), jnp.float32, -s, s)
        Wv = jax.random.uniform(ks[5], (HIDDEN, HIDDEN), jnp.float32, -s, s)
        bv = jax.random.uniform(ks[6], (HIDDEN,), jnp.float32, -s, s)
        Wo = jax.random.uniform(ks[7], (HIDDEN, HIDDEN), jnp.float32, -s, s)
        bo = jax.random.uniform(ks[8], (HIDDEN,), jnp.float32, -s, s)
        return {'x': x, 'Wq': Wq, 'bq': bq, 'Wk': Wk, 'bk': bk, 'Wv': Wv, 'bv': bv, 'Wo': Wo, 'bo': bo}
    _L0_attn_in = _L0_attn_setup()

    def _L0_ffn_setup():
        import jax, jax.numpy as jnp
        import numpy as np
        DIM = 128
        DEPTH = 2
        HEADS = 8
        DIM_HEAD = 64
        WINDOW = 64
        INNER = HEADS * DIM_HEAD
        HID = int(DIM * 4 * 2 / 3)
        B, N = (2, 1024)
        QK_SCALE = 8.0

        def shift_token(t):
            t1, t2 = jnp.split(t, 2, axis=-1)
            t2 = jnp.pad(t2, ((0, 0), (1, 0), (0, 0)))[:, :-1]
            return jnp.concatenate([t1, t2], axis=-1)

        def l2norm(t):
            return t / jnp.clip(jnp.linalg.norm(t, axis=-1, keepdims=True), 1e-12)

        def rotate_half(x):
            x1, x2 = jnp.split(x, 2, axis=-1)
            return jnp.concatenate([-x2, x1], axis=-1)

        def rotary_xpos(q, k):
            n = q.shape[-2]
            half_idx = jnp.arange(0, DIM_HEAD, 2, dtype=jnp.float32)
            inv_freq = 1.0 / 10000.0 ** (half_idx / DIM_HEAD)
            t = jnp.arange(n, dtype=jnp.float32)
            freqs = t[:, None] * inv_freq[None, :]
            freqs = jnp.concatenate([freqs, freqs], axis=-1)
            base = (half_idx + 0.4 * DIM_HEAD) / (1.4 * DIM_HEAD)
            power = (t - n // 2) / float(WINDOW // 2)
            scale = base[None, :] ** power[:, None]
            scale = jnp.concatenate([scale, scale], axis=-1)
            cos, sin = (jnp.cos(freqs), jnp.sin(freqs))
            q = q * cos * scale + rotate_half(q) * sin * scale
            k = k * cos / scale + rotate_half(k) * sin / scale
            return (q, k)

        def local_attention(q, k, v):
            b, h, n, d = q.shape
            w = n // WINDOW
            bq = q.reshape(b, h, w, WINDOW, d) * QK_SCALE
            bk = k.reshape(b, h, w, WINDOW, d)
            bv = v.reshape(b, h, w, WINDOW, d)

            def look_around(t):
                p = jnp.pad(t, ((0, 0), (0, 0), (1, 0), (0, 0), (0, 0)))
                return jnp.concatenate([p[:, :, :w], p[:, :, 1:]], axis=3)
            bk, bv = (look_around(bk), look_around(bv))
            bt = jnp.arange(n).reshape(w, WINDOW)
            btp = jnp.pad(bt, ((1, 0), (0, 0)), constant_values=-1)
            btk = jnp.concatenate([btp[:w], btp[1:]], axis=1)
            sim = jnp.einsum('bhwid,bhwjd->bhwij', bq, bk)
            i = bt[:, :, None]
            j = btk[:, None, :]
            mask = (i < j) | (i > j + WINDOW) | (j == -1)
            sim = jnp.where(mask, -jnp.finfo(sim.dtype).max, sim)
            attn = jax.nn.softmax(sim, axis=-1)
            out = jnp.einsum('bhwij,bhwjd->bhwid', attn, bv)
            return out.reshape(b, h, n, d)

        def _layer(x, wqkv, qs, ksc, wo, lg, lb, w1, b1, w2, b2):
            b, n, _ = x.shape
            h = shift_token(x)
            qkv = h @ wqkv
            q, k, v = jnp.split(qkv, 3, axis=-1)
            to_heads = lambda t: t.reshape(b, n, HEADS, DIM_HEAD).transpose(0, 2, 1, 3)
            q, k, v = (to_heads(q), to_heads(k), to_heads(v))
            q = l2norm(q) * qs
            k = l2norm(k) * ksc
            q, k = rotary_xpos(q, k)
            o = local_attention(q, k, v)
            o = o.transpose(0, 2, 1, 3).reshape(b, n, INNER)
            x = x + o @ wo
            h = shift_token(x)
            mu = h.mean(-1, keepdims=True)
            var = h.var(-1, keepdims=True)
            h = (h - mu) / jnp.sqrt(var + 1e-05) * lg + lb
            h = h @ w1 + b1
            a, g = jnp.split(h, 2, axis=-1)
            h = a * jax.nn.gelu(g, approximate=False)
            x = x + h @ w2 + b2
            return x
        key = jax.random.key(seed)
        ks = jax.random.split(key, 6)
        return {'x': jax.random.normal(ks[0], (B, N, DIM), jnp.float32), 'wqkv': jax.random.normal(ks[1], (DEPTH, DIM, 3 * INNER), jnp.float32) * 0.02, 'q_scale': jnp.ones((DEPTH, DIM_HEAD), jnp.float32), 'k_scale': jnp.ones((DEPTH, DIM_HEAD), jnp.float32), 'wo': jax.random.normal(ks[2], (DEPTH, INNER, DIM), jnp.float32) * 0.02, 'ln_g': jnp.ones((DEPTH, DIM), jnp.float32), 'ln_b': jnp.zeros((DEPTH, DIM), jnp.float32), 'w1': jax.random.normal(ks[3], (DEPTH, DIM, 2 * HID), jnp.float32) * 0.02, 'b1': jnp.zeros((DEPTH, 2 * HID), jnp.float32), 'w2': jax.random.normal(ks[4], (DEPTH, HID, DIM), jnp.float32) * 0.02, 'b2': jnp.zeros((DEPTH, DIM), jnp.float32)}
    _L0_ffn_in = _L0_ffn_setup()
    _L0_c = _w((lambda *s: np.random.randn(*s).astype(np.float32) * 0.05)(4, 128))
    _L0_wmod = _w((lambda *s: np.random.randn(*s).astype(np.float32) * 0.05)(128, 6 * 128) * 128 ** (-0.5))
    _d = {'L0_attn_x': _L0_attn_in['x'], 'L0_attn_Wq': _L0_attn_in['Wq'], 'L0_attn_bq': _L0_attn_in['bq'], 'L0_attn_Wk': _L0_attn_in['Wk'], 'L0_attn_bk': _L0_attn_in['bk'], 'L0_attn_Wv': _L0_attn_in['Wv'], 'L0_attn_bv': _L0_attn_in['bv'], 'L0_attn_Wo': _L0_attn_in['Wo'], 'L0_attn_bo': _L0_attn_in['bo'], 'L0_ffn_wqkv': _L0_ffn_in['wqkv'], 'L0_ffn_q_scale': _L0_ffn_in['q_scale'], 'L0_ffn_k_scale': _L0_ffn_in['k_scale'], 'L0_ffn_wo': _L0_ffn_in['wo'], 'L0_ffn_ln_g': _L0_ffn_in['ln_g'], 'L0_ffn_ln_b': _L0_ffn_in['ln_b'], 'L0_ffn_w1': _L0_ffn_in['w1'], 'L0_ffn_b1': _L0_ffn_in['b1'], 'L0_ffn_w2': _L0_ffn_in['w2'], 'L0_ffn_b2': _L0_ffn_in['b2'], 'L0_c': _L0_c, 'L0_wmod': _L0_wmod}
    _x0 = _d['L0_attn_x']
    _d['L0_attn_x'] = jax.random.normal(jax.random.fold_in(jax.random.key(seed), 1), (4, 1024, 128), dtype=_x0.dtype)
    del _x0
    return _d

def reference(L0_attn_x, L0_attn_Wq, L0_attn_bq, L0_attn_Wk, L0_attn_bk, L0_attn_Wv, L0_attn_bv, L0_attn_Wo, L0_attn_bo, L0_ffn_wqkv, L0_ffn_q_scale, L0_ffn_k_scale, L0_ffn_wo, L0_ffn_ln_g, L0_ffn_ln_b, L0_ffn_w1, L0_ffn_b1, L0_ffn_w2, L0_ffn_b2, L0_c, L0_wmod):

    def _L0_attn_ref(x, Wq, bq, Wk, bk, Wv, bv, Wo, bo):
        import jax, jax.numpy as jnp
        import numpy as np
        HIDDEN = 128
        HEADS = 16
        HEAD_DIM = HIDDEN // HEADS
        bs, seq_len, _ = x.shape

        def proj(W, b):
            y = x @ W + b
            return y.reshape(bs, seq_len, HEADS, HEAD_DIM).transpose(0, 2, 1, 3)
        q = proj(Wq, bq)
        k = proj(Wk, bk)
        v = proj(Wv, bv)
        scale = 1.0 / jnp.sqrt(jnp.float32(HEAD_DIM))
        scores = jnp.einsum('bhqd,bhkd->bhqk', q, k) * scale
        attn = jax.nn.softmax(scores, axis=-1)
        ctx = jnp.einsum('bhqk,bhkd->bhqd', attn, v)
        ctx = ctx.transpose(0, 2, 1, 3).reshape(bs, seq_len, HIDDEN)
        return ctx @ Wo + bo

    def _L0_ffn_ref(x, wqkv, q_scale, k_scale, wo, ln_g, ln_b, w1, b1, w2, b2):
        import jax, jax.numpy as jnp
        import numpy as np
        DIM = 128
        DEPTH = 2
        HEADS = 8
        DIM_HEAD = 64
        WINDOW = 64
        INNER = HEADS * DIM_HEAD
        HID = int(DIM * 4 * 2 / 3)
        B, N = (2, 1024)
        QK_SCALE = 8.0

        def shift_token(t):
            t1, t2 = jnp.split(t, 2, axis=-1)
            t2 = jnp.pad(t2, ((0, 0), (1, 0), (0, 0)))[:, :-1]
            return jnp.concatenate([t1, t2], axis=-1)

        def l2norm(t):
            return t / jnp.clip(jnp.linalg.norm(t, axis=-1, keepdims=True), 1e-12)

        def rotate_half(x):
            x1, x2 = jnp.split(x, 2, axis=-1)
            return jnp.concatenate([-x2, x1], axis=-1)

        def rotary_xpos(q, k):
            n = q.shape[-2]
            half_idx = jnp.arange(0, DIM_HEAD, 2, dtype=jnp.float32)
            inv_freq = 1.0 / 10000.0 ** (half_idx / DIM_HEAD)
            t = jnp.arange(n, dtype=jnp.float32)
            freqs = t[:, None] * inv_freq[None, :]
            freqs = jnp.concatenate([freqs, freqs], axis=-1)
            base = (half_idx + 0.4 * DIM_HEAD) / (1.4 * DIM_HEAD)
            power = (t - n // 2) / float(WINDOW // 2)
            scale = base[None, :] ** power[:, None]
            scale = jnp.concatenate([scale, scale], axis=-1)
            cos, sin = (jnp.cos(freqs), jnp.sin(freqs))
            q = q * cos * scale + rotate_half(q) * sin * scale
            k = k * cos / scale + rotate_half(k) * sin / scale
            return (q, k)

        def local_attention(q, k, v):
            b, h, n, d = q.shape
            w = n // WINDOW
            bq = q.reshape(b, h, w, WINDOW, d) * QK_SCALE
            bk = k.reshape(b, h, w, WINDOW, d)
            bv = v.reshape(b, h, w, WINDOW, d)

            def look_around(t):
                p = jnp.pad(t, ((0, 0), (0, 0), (1, 0), (0, 0), (0, 0)))
                return jnp.concatenate([p[:, :, :w], p[:, :, 1:]], axis=3)
            bk, bv = (look_around(bk), look_around(bv))
            bt = jnp.arange(n).reshape(w, WINDOW)
            btp = jnp.pad(bt, ((1, 0), (0, 0)), constant_values=-1)
            btk = jnp.concatenate([btp[:w], btp[1:]], axis=1)
            sim = jnp.einsum('bhwid,bhwjd->bhwij', bq, bk)
            i = bt[:, :, None]
            j = btk[:, None, :]
            mask = (i < j) | (i > j + WINDOW) | (j == -1)
            sim = jnp.where(mask, -jnp.finfo(sim.dtype).max, sim)
            attn = jax.nn.softmax(sim, axis=-1)
            out = jnp.einsum('bhwij,bhwjd->bhwid', attn, bv)
            return out.reshape(b, h, n, d)

        def _layer(x, wqkv, qs, ksc, wo, lg, lb, w1, b1, w2, b2):
            b, n, _ = x.shape
            h = shift_token(x)
            qkv = h @ wqkv
            q, k, v = jnp.split(qkv, 3, axis=-1)
            to_heads = lambda t: t.reshape(b, n, HEADS, DIM_HEAD).transpose(0, 2, 1, 3)
            q, k, v = (to_heads(q), to_heads(k), to_heads(v))
            q = l2norm(q) * qs
            k = l2norm(k) * ksc
            q, k = rotary_xpos(q, k)
            o = local_attention(q, k, v)
            o = o.transpose(0, 2, 1, 3).reshape(b, n, INNER)
            x = x + o @ wo
            h = shift_token(x)
            mu = h.mean(-1, keepdims=True)
            var = h.var(-1, keepdims=True)
            h = (h - mu) / jnp.sqrt(var + 1e-05) * lg + lb
            h = h @ w1 + b1
            a, g = jnp.split(h, 2, axis=-1)
            h = a * jax.nn.gelu(g, approximate=False)
            x = x + h @ w2 + b2
            return x
        for l in range(DEPTH):
            x = _layer(x, wqkv[l], q_scale[l], k_scale[l], wo[l], ln_g[l], ln_b[l], w1[l], b1[l], w2[l], b2[l])
        return x
    x = L0_attn_x
    mod = (_silu(L0_c) @ L0_wmod).reshape(L0_c.shape[0], 6, 1, -1)
    sa, ca, ga, sb, cb, gb = (mod[:, 0], mod[:, 1], mod[:, 2], mod[:, 3], mod[:, 4], mod[:, 5])
    ga = (2 * (ga >= 0) - 1) * jnp.maximum(jnp.abs(ga), 0.25)
    gb = (2 * (gb >= 0) - 1) * jnp.maximum(jnp.abs(gb), 0.25)
    h = _layernorm(x, axis=-1) * (1 + ca) + sa
    x = x + ga * _L0_attn_ref(h, L0_attn_Wq, L0_attn_bq, L0_attn_Wk, L0_attn_bk, L0_attn_Wv, L0_attn_bv, L0_attn_Wo, L0_attn_bo)
    h = _layernorm(x, axis=-1) * (1 + cb) + sb
    x = x + gb * _L0_ffn_ref(h, L0_ffn_wqkv, L0_ffn_q_scale, L0_ffn_k_scale, L0_ffn_wo, L0_ffn_ln_g, L0_ffn_ln_b, L0_ffn_w1, L0_ffn_b1, L0_ffn_w2, L0_ffn_b2)
    return x

_drawn_inputs = setup_inputs


def setup_inputs(seed=0):
    import zlib

    import numpy as np

    out = dict(_drawn_inputs(seed))
    spreads = {'L0_ffn_q_scale': (1.0, 0.6),
     'L0_ffn_k_scale': (1.0, 0.6),
     'L0_ffn_ln_g': (1.0, 0.6),
     'L0_ffn_ln_b': (0.0, 0.8),
     'L0_ffn_b1': (0.0, 0.8),
     'L0_ffn_b2': (0.0, 0.8)}
    factors = {'L0_attn_Wq': 8.0,
     'L0_attn_bq': 8.0,
     'L0_attn_Wk': 8.0,
     'L0_attn_bk': 64.0,
     'L0_attn_Wv': 8.0,
     'L0_attn_bv': 6.808,
     'L0_attn_Wo': 6.676,
     'L0_attn_bo': 4.331,
     'L0_ffn_wqkv': 8.0,
     'L0_ffn_wo': 8.0,
     'L0_ffn_w1': 8.0,
     'L0_ffn_w2': 8.0}
    for name, (base, spread) in spreads.items():
        noise = np.random.default_rng([zlib.crc32(name.encode()), seed]).standard_normal(out[name].shape)
        drawn = base * np.exp(spread * noise) if base else spread * noise
        out[name] = jnp.asarray(drawn.astype(out[name].dtype))
    for name, factor in factors.items():
        out[name] = (out[name] * factor).astype(out[name].dtype)
    return out
```

```python
from contextlib import ExitStack

import numpy as np

import concourse.bass as bass
from concourse import mybir

F32 = mybir.dt.float32
BF16 = mybir.dt.bfloat16
ALU = mybir.AluOpType
ACT = mybir.ActivationFunctionType
AX = mybir.AxisListType

P = 128
B, N, D = 4, 1024, 128
H, HD = 16, 8
TOK = B * N
CH = 512
NCH = TOK // CH
TPC = CH // P
TPB = N // P
GH = 4
NG = H // GH
PAIRS = H // 2
QROWS = (0, 1, 2, 0, 1, 0)
KROWS = (0, 0, 0, 1, 1, 2)
SROWS = HD * len(QROWS)
MROWS = 3
PROWS = 2 * SROWS
STACK = PROWS + 2 * MROWS
VW = 2 * HD
ATT_SCALE = float(1.0 / np.sqrt(np.float32(HD)))
EPS = 1e-5

LH, LD = 8, 64
INNER = LH * LD
WINDOW = 64
HID = 341
HCH = ((0, 128), (128, 128), (256, HID - 256))
DEPTH = 2
TILES = DEPTH * B * TPB
CHUNKS = DEPTH * NCH
QK_SCALE = 8.0
NORM_SHIFT = 16


TABLE_SET = "natural_log_exp_and_others"
SAVE_INC = 16 * 2 * len(QROWS)
FILL_INC = 16 * 4


def fill_stack(sp, t, b, j):
    for w, (name, step) in enumerate((("q_stack", 1), ("k_stack", 2))):
        for par in range(2):
            first = 2 * j if w == 0 else GH * j + par
            src = t["part_rows"][w, :, :, :, bass.ds(b * N, N)].rearrange(
                "(p a) r d n -> a p (r d) n", a=2)[par, 2 * j:2 * j + 2].rearrange("p r n -> r p n")
            dst = t[name][SROWS * par:SROWS * (par + 1), first:first + step + 1:step, :]
            sp.dma_start(dst, src).then_inc(t["stacked"][j], 16)


def prep_phase(nc, t, dram):
    with ExitStack() as ctx:
        def sb(name, shape, dt=F32):
            return ctx.enter_context(nc.sbuf_tensor(name, shape, dt))

        def sem(name):
            return ctx.enter_context(nc.semaphore(name))

        x_tok = sb("x_tok", [P, 2, TPC, D])
        rstd = sb("a_rstd", [P, 2, CH])
        h_mod = sb("a_h_mod", [P, 2, CH])
        rest = sb("a_rest", [P, 2, 2, CH])
        silu_c = sb("silu_c", [P, B])
        c_exp = sb("c_exp", [P, B])
        c_den = sb("c_den", [P, B])
        c_rec = sb("c_rec", [P, B])
        gate_sign = sb("gate_sign", [P, 2, B])
        gate_neg = sb("gate_neg", [P, 2, B])
        gate_abs = sb("gate_abs", [P, 2, B])
        banks = [ctx.enter_context(nc.psum_tensor(f"prep{i}", [P, CH], F32)) for i in range(7)]
        bank_xq, bank_cv, bank_vk, ps_mod = banks[0:2], banks[2:4], banks[4:6], banks[6]

        const_loaded = sem("const_loaded")
        x_loaded = [sem(f"x_loaded{i}") for i in range(2)]
        gp = sem("gp_consts")
        k_clear = sem("k_clear")
        silu_step = sem("silu_step")
        c_exp_ready = sem("c_exp_ready")
        mod_ready = sem("mod_ready")
        mod_step = sem("mod_step")
        bias_ready = sem("bias_ready")
        x_turned = sem("x_turned")
        x_kept = sem("x_kept")
        centred = sem("centred")
        squared = sem("squared")
        var_ready = sem("var_ready")
        log_ready = sem("log_ready")
        rstd_ready = sem("rstd_ready")
        normed_ready = sem("normed_ready")
        h_ready = sem("h_ready")
        qk_ready = sem("qk_ready")
        v_ready = sem("v_ready")
        high_ready = sem("high_ready")
        rest_ready = sem("rest_ready")
        mid_ready = sem("mid_ready")
        low_ready = sem("low_ready")
        v_kept = sem("v_kept")
        block = ctx.enter_context(nc.Block())

        x_dram = dram["L0_attn_x"].rearrange("b (t p) d -> p (b t) d", p=P)
        consts = [
            (t["wmod"][:, :], dram["L0_wmod"]),
            (t["c_t"][:, :], dram["L0_c"].rearrange("b d -> d b")),
            (t["identity"][:, :], dram["identity"]),
            (t["center"][:, :], dram["center"]),
            (t["wq"][:, :], dram["L0_attn_Wq"]),
            (t["wk"][:, :], dram["L0_attn_Wk"]),
            (t["wv"][:, :], dram["L0_attn_Wv"]),
            (t["wo"][:, :], dram["L0_attn_Wo"]),
        ] + [(t["bias4"][:, i:i + 1], dram[f"L0_attn_{n}"].rearrange("(p a) -> p a", a=1))
             for i, n in enumerate(("bq", "bk", "bv", "bo"))]

        @block.sync
        def _(sp):
            for i in range(2):
                sp.dma_start(x_tok[:, i], x_dram[:, i * TPC:(i + 1) * TPC, :]).then_inc(x_loaded[i], 16)
            for dst, src in consts:
                sp.dma_start(dst, src, allow_slow_non_contiguous=True).then_inc(const_loaded, 16)

            def next_x(b):
                for i in range(2):
                    sp.wait_ge(x_turned, 2 * b + (i - 1))
                    sp.dma_start(x_tok[:, i], x_dram[:, bass.ds((2 * b + i) * TPC, TPC), :]
                                 ).then_inc(x_loaded[i], 16)

            def save_parts(b):
                sp.wait_ge(low_ready, 4 * b + 4)
                for w, rows in enumerate((QROWS, KROWS)):
                    for r, part in enumerate(rows):
                        sp.dma_start(t["part_rows"][w, :, r, :, bass.ds(b * N, N)],
                                     t["qk_parts"][:, w, part, bass.ds(b * N, N)]).then_inc(t["parts_saved"], 16)

            next_x(1)
            save_parts(0)
            sp.wait_ge(t["parts_saved"], SAVE_INC)
            sp.wait_ge(k_clear, 4)
            for j in range(NG):
                fill_stack(sp, t, 0, j)
            with sp.Fori(1, B - 1) as b:
                next_x(b + 1)
                save_parts(b)
            save_parts(B - 1)

        @block.gpsimd
        def _(pool):
            nc.gpsimd.memset(t["mean"][:, :], 1.0 / D).then_inc(gp, 1)
            nc.gpsimd.memset(t["v_slots"][:, :, :, :, HD:VW], 1.0).then_inc(gp, 1)
            nc.gpsimd.memset(t["eps_col"][:, :], EPS).then_inc(gp, 1)
            k_words = t["k_stack"][:, :, :].rearrange("p h n -> p (h n)").bitcast(mybir.dt.uint32)
            nc.gpsimd.memset(k_words, 0).then_inc(k_clear, 1)
            pool.wait_ge(k_clear, 1)
            nc.gpsimd.memset(t["k_stack"][PROWS:STACK, 1::2, :], 1.0).then_inc(k_clear, 1)
            pool.wait_ge(k_clear, 2)
            nc.gpsimd.memset(t["k_stack"][PROWS:PROWS + MROWS, 1::2, :], 0.0).then_inc(k_clear, 1)
            pool.wait_ge(k_clear, 3)
            nc.gpsimd.memset(t["k_stack"][PROWS:PROWS + MROWS, 0::2, :], 1.0).then_inc(k_clear, 1)
            pool.wait_ge(k_clear, 4)
            with pool.Fori(0, B) as b:
                for i in range(2):
                    for w in range(2):
                        where = bass.ds((2 * b + i) * CH, CH)
                        mid, low = t["qk_parts"][:, w, 1, where], t["qk_parts"][:, w, 2, where]
                        pool.wait_ge(rest_ready, 4 * b + (2 * i + w + 1))
                        nc.gpsimd.tensor_copy(mid, rest[:, i, w]).then_inc(mid_ready, 1)
                        pool.wait_ge(mid_ready, 4 * b + (2 * i + w + 1))
                        nc.gpsimd.tensor_tensor(low, rest[:, i, w], mid, ALU.subtract).then_inc(low_ready, 1)

        @block.scalar
        def _(act):
            nc.scalar.preload_act_table_set(TABLE_SET)
            act.wait_ge(const_loaded, 16 * len(consts))
            nc.scalar.activation(c_exp[:, :], t["c_t"][:, :], ACT.Exp, scale=-1.0).then_inc(c_exp_ready, 1)
            act.wait_ge(gp, 3)
            with act.Fori(0, B) as b:
                for i in range(2):
                    act.wait_ge(centred, 2 * b + (i + 1))
                    nc.scalar.activation(rstd[:, i], bank_cv[i][:, :], ACT.Square).then_inc(squared, 1)
                for i in range(2):
                    act.wait_ge(var_ready, 2 * b + (i + 1))
                    nc.scalar.activation(rstd[:, i], bank_vk[i][:, :], ACT.Ln, bias=t["eps_col"][:, :]
                                         ).then_inc(log_ready, 1)
                    act.wait_ge(log_ready, 2 * b + (i + 1))
                    nc.scalar.activation(rstd[:, i], rstd[:, i], ACT.Exp, scale=-0.5).then_inc(rstd_ready, 1)
                for i in range(2):
                    for w, bank in enumerate((bank_xq[i], bank_vk[i])):
                        act.wait_ge(qk_ready, 4 * b + (2 * i + w + 1))
                        nc.scalar.activation(t["qk_parts"][:, w, 0, bass.ds((2 * b + i) * CH, CH)], bank[:, :],
                                             ACT.Identity, bias=t["bias4"][:, w:w + 1]).then_inc(high_ready, 1)

        @block.vector
        def _(dve):
            dve.wait_ge(c_exp_ready, 1)
            nc.vector.tensor_scalar(c_den[:, :], c_exp[:, :], 1.0, None, ALU.add).then_inc(silu_step, 1)
            dve.wait_ge(silu_step, 1)
            nc.vector.reciprocal(c_rec[:, :], c_den[:, :]).then_inc(silu_step, 1)
            dve.wait_ge(silu_step, 2)
            nc.vector.tensor_tensor(silu_c[:, :], t["c_t"][:, :], c_rec[:, :], ALU.mult).then_inc(silu_step, 1)
            nc.vector.tensor_copy(t["identity_bf"][:, :], t["identity"][:, :])
            dve.wait_ge(mod_ready, 1)
            mod = t["mod"]
            nc.vector.tensor_copy(mod[:, :, :], ps_mod[:, 0:6 * B].rearrange("p (s b) -> p s b", b=B)
                                  ).then_inc(mod_step, 1)
            nc.vector.tensor_tensor(t["wo_bv"][:, :], ps_mod[:, 6 * B:6 * B + 1], t["bias4"][:, 3:4], ALU.add
                                    ).then_inc(mod_step, 1)
            dve.wait_ge(mod_step, 2)
            for s in (1, 4):
                nc.vector.tensor_scalar(mod[:, s, :], mod[:, s, :], 1.0, None, ALU.add).then_inc(mod_step, 1)
            for n, s in enumerate((2, 5)):
                nc.vector.tensor_scalar(gate_sign[:, n], mod[:, s, :], 0.0, 2.0, ALU.is_ge, ALU.mult
                                        ).then_inc(mod_step, 1)
                nc.vector.tensor_scalar(gate_neg[:, n], mod[:, s, :], -1.0, 0.25, ALU.mult, ALU.max
                                        ).then_inc(mod_step, 1)
            dve.wait_ge(mod_step, 8)
            for n, s in enumerate((2, 5)):
                nc.vector.tensor_tensor(gate_abs[:, n], mod[:, s, :], gate_neg[:, n], ALU.max).then_inc(mod_step, 1)
            dve.wait_ge(mod_step, 10)
            for n, s in enumerate((2, 5)):
                nc.vector.scalar_tensor_tensor(out=mod[:, s, :], in0=gate_sign[:, n], scalar=-1.0,
                                               in1=gate_abs[:, n], op0=ALU.add, op1=ALU.mult).then_inc(mod_step, 1)
            dve.wait_ge(mod_step, 12)
            nc.vector.tensor_scalar(t["ga_bias"][:, :], mod[:, 2, :], t["wo_bv"][:, 0:1], None, ALU.mult
                                    ).then_inc(bias_ready, 1)
            with dve.Fori(0, B) as b:
                for i in range(2):
                    dve.wait_ge(x_turned, 2 * b + (i + 1))
                    nc.vector.tensor_copy(t["x_t"][:, bass.ds((2 * b + i) * CH, CH)], bank_xq[i][:, :]
                                          ).then_inc(x_kept, 1)
                for i in range(2):
                    dve.wait_ge(rstd_ready, 2 * b + (i + 1))
                    nc.vector.tensor_tensor(h_mod[:, i], bank_cv[i][:, :], rstd[:, i], ALU.mult
                                            ).then_inc(normed_ready, 1)
                    dve.wait_ge(normed_ready, 2 * b + (i + 1))
                    nc.vector.tensor_scalar(h_mod[:, i], h_mod[:, i], mod[:, 1, bass.ds(b, 1)],
                                            mod[:, 0, bass.ds(b, 1)], ALU.mult, ALU.add).then_inc(h_ready, 1)
                for i in range(2):
                    dve.wait_ge(v_ready, 2 * b + (i + 1))
                    nc.vector.tensor_copy(t["v_all"][:, bass.ds((2 * b + i) * TPC, TPC), :],
                                          bank_cv[i][:, :].rearrange("p (t f) -> p t f", t=TPC)).then_inc(v_kept, 1)
                    for w, bank in enumerate((bank_xq[i], bank_vk[i])):
                        dve.wait_ge(high_ready, 4 * b + (2 * i + w + 1))
                        nc.vector.scalar_tensor_tensor(out=rest[:, i, w], in0=bank[:, :],
                                                       scalar=t["bias4"][:, w:w + 1],
                                                       in1=t["qk_parts"][:, w, 0, bass.ds((2 * b + i) * CH, CH)],
                                                       op0=ALU.add, op1=ALU.subtract).then_inc(rest_ready, 1)
                dve.wait_ge(low_ready, 4 * b + 4)

        @block.tensor
        def _(pe):
            pe.wait_ge(const_loaded, 16 * len(consts))
            pe.wait_ge(silu_step, 3)
            for s in range(6):
                nc.tensor.matmul(ps_mod[:, s * B:(s + 1) * B], t["wmod"][:, s * D:(s + 1) * D], silu_c[:, :],
                                 start=True, stop=True)
            nc.tensor.matmul(ps_mod[:, 6 * B:6 * B + 1], t["wo"][:, :], t["bias4"][:, 2:3],
                             start=True, stop=True).then_inc(mod_ready, 1)
            pe.wait_ge(gp, 3)
            with pe.Fori(0, B) as b:
                for i in range(2):
                    pe.wait_ge(x_loaded[i], 16 * b + 16)
                    for k in range(TPC):
                        mm = nc.tensor.transpose(bank_xq[i][:, k * P:(k + 1) * P], x_tok[:, i, k, :],
                                                 t["identity"][:, :])
                    mm.then_inc(x_turned, 1)
                for i in range(2):
                    pe.wait_ge(x_kept, 2 * b + (i + 1))
                    nc.tensor.matmul(bank_cv[i][:, :], t["center"][:, :], t["x_t"][:, bass.ds((2 * b + i) * CH, CH)],
                                     start=True, stop=True).then_inc(centred, 1)
                for i in range(2):
                    pe.wait_ge(squared, 2 * b + (i + 1))
                    nc.tensor.matmul(bank_vk[i][:, :], t["mean"][:, :], rstd[:, i], start=True, stop=True
                                     ).then_inc(var_ready, 1)
                for i in range(2):
                    pe.wait_ge(h_ready, 2 * b + (i + 1))
                    pe.wait_ge(rstd_ready, 2 * b + (i + 1))
                    for k in range(TPC):
                        mm = nc.tensor.matmul(bank_cv[i][:, k * P:(k + 1) * P], h_mod[:, i, k * P:(k + 1) * P],
                                              t["wv"][:, :], start=True, stop=True)
                    mm.then_inc(v_ready, 1)
                    nc.tensor.matmul(bank_xq[i][:, :], t["wq"][:, :], h_mod[:, i], start=True, stop=True
                                     ).then_inc(qk_ready, 1)
                    nc.tensor.matmul(bank_vk[i][:, :], t["wk"][:, :], h_mod[:, i], start=True, stop=True
                                     ).then_inc(qk_ready, 1)
                pe.wait_ge(v_kept, 2 * b + 2)
                pe.wait_ge(rest_ready, 4 * b + 4)


def attention_phase(nc, t, dram):
    KT = N // P
    QT = CH // P
    UNITS = 2 * KT * GH
    BLOCKS = 2 * KT
    POS = QT * GH + 1
    TURN = 2
    AHEAD = (0, 3, 1, 0)
    ROWS_INC = 16 * 2
    OUT_INC = 16

    with ExitStack() as ctx:
        def sb(name, shape, dt=F32):
            return ctx.enter_context(nc.sbuf_tensor(name, shape, dt))

        def sem(name):
            return ctx.enter_context(nc.semaphore(name))

        probs = sb("probs", [P, 2, GH, CH])
        row_max, max_rest, zeros, max_parts, max_rows = (t[name] for name in (
            "row_max", "max_rest", "zeros", "max_parts", "max_rows"))
        rope = sb("rope", [P, 2, TPB, 2, LD])
        scales = sb("scales", [P, 2, 2, DEPTH, LD])
        masks_in = sb("masks_in", [P, 2 * P])
        head_out = sb("head_out", [P, 2, CH])
        ps_max = [ctx.enter_context(nc.psum_tensor(f"ps_max{i}", [P, N], F32)) for i in range(2)]
        ps_score = [ctx.enter_context(nc.psum_tensor(f"ps_score{i}", [P, CH], F32)) for i in range(2)]
        ps_out = [ctx.enter_context(nc.psum_tensor(f"ps_out{i}", [P, CH], F32)) for i in range(2)]

        loaded = sem("f_loaded")
        table_ready = sem("table_ready")
        stacked = t["stacked"]
        v_placed = [sem(f"v_placed{j}") for j in range(NG)]
        max_scores = sem("max_scores")
        max_taken = sem("max_taken")
        zeros_set = sem("zeros_set")
        part_step = sem("part_step")
        parts_ready = sem("parts_ready")
        rows_placed = [sem(f"rows_placed{c}") for c in range(2)]
        out_placed = [sem(f"out_placed{c}") for c in range(2)]
        probs_ready = sem("probs_ready")
        values_done = sem("values_done")
        out_kept = sem("out_kept")
        scores_ready = sem("scores_ready")
        block = ctx.enter_context(nc.Block())

        def positions(first, last):
            for c in range(2):
                for k in range(POS):
                    turn = k == TURN and not (first and c == 0)
                    if (k == TURN and not turn) or (last and not (turn and c == 0)):
                        continue
                    yield c, None if turn else k - (k > TURN), POS * c + k

        def taken(g, p, first=False, last=False):
            if last:
                return 2 * POS * g
            return p + 1 if first and p < TURN else 2 * POS * g + p

        def rows_turned(g, c, last=False):
            return taken(g + 1, TURN, last=last) if c else taken(g, POS + TURN)

        LOADS = [(t["wqkv"][:, :, :], dram["L0_ffn_wqkv"].rearrange("l p n -> p l n")),
                 (t["wout"][:, :, :, :].rearrange("p l c n -> p (l c) n"),
                  dram["L0_ffn_wo"].rearrange("l (c p) n -> p (l c) n", p=P)),
                 (t["w1"][:, :, :], dram["L0_ffn_w1"].rearrange("l p n -> p l n")),
                 (rope[:, :, :, :, :].rearrange("p a t w d -> p (a t w d)"), dram["rope"]),
                 (masks_in[:, :], dram["masks"]),
                 (t["b2"][:, :], dram["L0_ffn_b2"].rearrange("l p -> p l")),
                 (t["ln_g"][:, :], dram["L0_ffn_ln_g"].rearrange("l p -> p l")),
                 (t["ln_b"][:, :], dram["L0_ffn_ln_b"].rearrange("l p -> p l"))]
        for c, (at, n) in enumerate(HCH):
            LOADS.append((t["w2"][0:n, :, c], dram["L0_ffn_w2"][:, at:at + n].rearrange("l p n -> p l n")))
            for k in range(2):
                LOADS.append((t["b1"][0:n, :, k, c],
                              dram["L0_ffn_b1"][:, HID * k + at:HID * k + at + n].rearrange("l p -> p l")))
        for w, name in enumerate(("L0_ffn_q_scale", "L0_ffn_k_scale")):
            src = dram[name].rearrange("(a l) d -> a l d", a=1)
            for swapped, to, at, n in ((0, 0, 0, LD), (1, 0, LD // 2, LD // 2), (1, LD // 2, 0, LD // 2)):
                LOADS.append((scales[:, w, swapped, :, to:to + n], src[:, :, at:at + n].broadcast_to((P, DEPTH, n))))

        @block.sync
        def _(sp):
            sp.wait_ge(t["parts_saved"], SAVE_INC * B)
            for dst, src in LOADS:
                sp.dma_start(dst, src, allow_slow_non_contiguous=True).then_inc(loaded, 16)

            def place_rows(g, j, c, last=False):
                sp.wait_ge(max_taken, rows_turned(g, c, last))
                for p in range(2):
                    sp.dma_start(t["q_stack"][PROWS:STACK, 2 * j + p, c * CH:(c + 1) * CH],
                                 max_rows[2 * MROWS * p:2 * MROWS * (p + 1), c, :]).then_inc(rows_placed[c], 16)

            def place_out(b, g, j, c):
                sp.wait_ge(out_kept, 2 * g + (c + 3))
                sp.dma_start(t["head_rows"][j, :, bass.ds(b * N + c * CH, CH)], head_out[:, c, :]
                             ).then_inc(out_placed[c], 16)

            place_rows(0, 0, 0)

            def batch(b, last):
                for j in range(NG):
                    g = NG * b + j
                    final = last and j == NG - 1
                    place_rows(g, j, 1, final)
                    if not final:
                        place_rows(g + 1, (j + 1) % NG, 0)
                    place_out(b, g, j, 0)
                    place_out(b, g, j, 1)
                    if not last:
                        sp.wait_ge(scores_ready, UNITS * g + UNITS)
                        fill_stack(sp, t, b + 1, j)

            with sp.Fori(0, B - 1) as b:
                batch(b, False)
            batch(B - 1, True)
            for c in range(2):
                sp.wait_ge(out_placed[c], OUT_INC * NG * B + 1)

        @block.gpsimd
        def _(pool):
            def place_v(b, j):
                nc.gpsimd.tensor_copy(
                    t["v_slots"][:, j, :, :, 0:HD],
                    t["v_all"][:, bass.ds(b * TPB, TPB), GH * HD * j:GH * HD * (j + 1)]
                    .rearrange("p t (h d) -> p t h d", h=GH)).then_inc(v_placed[j], 1)

            def negative_parts(g, c, first=False):
                step = 4 * (2 * g + c)
                pool.wait_ge(max_taken, taken(g, POS * (c + 1) - 1, first))
                high, mid, low = (max_parts[:, c, :, :, k] for k in range(MROWS))
                nc.gpsimd.tensor_tensor(high, zeros[:, :, :], row_max[:, c], ALU.subtract).then_inc(part_step, 1)
                pool.wait_ge(part_step, step + 1)
                nc.gpsimd.tensor_tensor(max_rest[:, c], row_max[:, c], high, ALU.add).then_inc(part_step, 1)
                pool.wait_ge(part_step, step + 2)
                nc.gpsimd.tensor_tensor(mid, zeros[:, :, :], max_rest[:, c], ALU.subtract).then_inc(part_step, 1)
                pool.wait_ge(part_step, step + 3)
                nc.gpsimd.tensor_tensor(max_rest[:, c], max_rest[:, c], mid, ALU.add).then_inc(part_step, 1)
                pool.wait_ge(part_step, step + 4)
                nc.gpsimd.tensor_tensor(low, zeros[:, :, :], max_rest[:, c], ALU.subtract).then_inc(parts_ready, 1)

            nc.gpsimd.memset(zeros[:, :, :], 0.0).then_inc(zeros_set, 1)
            pool.wait_ge(zeros_set, 1)
            for j in range(NG):
                place_v(0, j)
            for c in range(2):
                negative_parts(0, c, True)
            pool.wait_ge(loaded, 16 * len(LOADS))
            nc.gpsimd.tensor_copy(t["masks"][:, :, :].rearrange("p a k -> p (a k)"), masks_in[:, :]
                                  ).then_inc(table_ready, 1)
            for l in range(DEPTH):
                for part in range(2):
                    for w in range(2):
                        nc.gpsimd.tensor_tensor(
                            t["table"][:, l, part, :, w, :], rope[:, part, :, w, :],
                            scales[:, w, part, l:l + 1, :].broadcast_to((P, TPB, LD)), ALU.mult
                        ).then_inc(table_ready, 1)

            def batch(b, last):
                for j in range(NG):
                    g = NG * b + j
                    if not (last and j == NG - 1):
                        for c in range(2):
                            negative_parts(g + 1, c)
                    if not last:
                        pool.wait_ge(values_done, BLOCKS * g + (BLOCKS + 2))
                        place_v(b + 1, j)

            with pool.Fori(0, B - 1) as b:
                batch(b, False)
            batch(B - 1, True)

        @block.scalar
        def _(act):
            nc.scalar.preload_act_table_set(TABLE_SET)
            act.sem_inc(values_done, 2)
            for c in range(2):
                act.sem_inc(out_placed[c], 1)

            def keep_out(g, c):
                act.wait_ge(values_done, BLOCKS * g + (KT * (c + 1) + 2))
                act.wait_ge(out_placed[c], OUT_INC * g + 1)
                nc.scalar.activation(head_out[:, c], ps_out[c][:, :], ACT.Copy).then_inc(out_kept, 1)

            def batch(b):
                for j in range(NG):
                    g = NG * b + j
                    for n in range(BLOCKS):
                        act.wait_ge(values_done, BLOCKS * g + (n + 1))
                        for h in range(GH):
                            u = GH * n + h
                            act.wait_ge(scores_ready, UNITS * g + (u + 1))
                            nc.scalar.activation(probs[:, n % 2, h], ps_score[u % 2][:, :], ACT.Exp,
                                                 scale=ATT_SCALE).then_inc(probs_ready, 1)
                        if n == KT:
                            keep_out(g, 0)
                    keep_out(g, 1)

            with act.Fori(0, B - 1) as b:
                batch(b)
            batch(B - 1)

        @block.vector
        def _(dve):
            for c in range(2):
                dve.sem_inc(rows_placed[c], 1)
                nc.vector.memset(ps_out[c][:, :], 0.0).then_inc(out_kept, 1)

            def first_pass(g, first=False, last=False):
                for c, k, p in positions(first, last):
                    dve.wait_ge(max_scores, taken(g, p, first, last))
                    if k is None:
                        turned = 1 - c
                        dve.wait_ge(rows_placed[turned], ROWS_INC * (g - turned) + 1)
                        nc.vector.tensor_copy(max_rows[:, turned, :],
                                              ps_max[p % 2][0:GH * MROWS, 0:CH // 2].bitcast(BF16)
                                              ).then_inc(max_taken, 1)
                    else:
                        if k == 0 and not first:
                            dve.wait_ge(parts_ready, 2 * g + (c - 1))
                        nc.vector.tensor_reduce(row_max[:, c, k // GH, k % GH:k % GH + 1], ps_max[p % 2][:, :],
                                                AX.X, ALU.max).then_inc(max_taken, 1)

            def batch(b, last):
                for j in range(NG):
                    g = NG * b + j
                    first_pass(g + 1, last=last and j == NG - 1)

            first_pass(0, first=True)
            with dve.Fori(0, B - 1) as b:
                batch(b, False)
            batch(B - 1, True)

        @block.tensor
        def _(pe):
            pe.sem_inc(probs_ready, 2)

            def first_pass(g, j, b, first=False, last=False):
                for c, k, p in positions(first, last):
                    bank = ps_max[p % 2]
                    if last:
                        pe.wait_ge(max_taken, 2 * POS * g - 1)
                    elif not first or p >= 2:
                        pe.wait_ge(max_taken, taken(g, p - 2, first))
                    if k is None:
                        turned = 1 - c
                        pe.wait_ge(parts_ready, 2 * g + (turned + 1 - 2 * turned))
                        for q in range(QT):
                            mm = nc.tensor.transpose(
                                bank[0:GH * MROWS, 0:CH // 2].bitcast(BF16)[:, q * P:(q + 1) * P],
                                max_parts[:, turned, q].rearrange("p h k -> p (h k)"), t["identity_bf"][:, :])
                    else:
                        if p == 0:
                            pe.wait_ge(stacked[j], FILL_INC * b + FILL_INC)
                        q, h = c * QT + k // GH, k % GH
                        for half in range(2):
                            mm = nc.tensor.matmul(bank[:, half * CH:(half + 1) * CH],
                                                  t["q_stack"][0:PROWS, 2 * j + h // 2, q * P:(q + 1) * P],
                                                  t["k_stack"][0:PROWS, GH * j + h, half * CH:(half + 1) * CH],
                                                  start=True, stop=True)
                            if half == 0:
                                yield
                    mm.then_inc(max_scores, 1)
                    yield

            def scores(g, j, n):
                c, k = divmod(n, KT)
                for h in range(GH):
                    u = GH * n + h
                    pe.wait_ge(probs_ready, UNITS * g + (u + 1))
                    nc.tensor.matmul(ps_score[u % 2][:, :],
                                     t["k_stack"][0:STACK, GH * j + h, k * P:(k + 1) * P],
                                     t["q_stack"][0:STACK, 2 * j + h // 2, c * CH:(c + 1) * CH],
                                     start=True, stop=True).then_inc(scores_ready, 1)
                    yield

            def values(g, j, n):
                c, k = divmod(n, KT)
                pe.wait_ge(probs_ready, UNITS * g + (GH * n + GH + 2))
                if k == 0:
                    pe.wait_ge(out_kept, 2 * g + (c + 1))
                for h in range(GH):
                    mm = nc.tensor.matmul(ps_out[c][32 * h:32 * h + VW, :], t["v_slots"][:, j, k, h, :],
                                          probs[:, n % 2, h], start=(k == 0), stop=(k == KT - 1))
                mm.then_inc(values_done, 1)

            def batch(b, last):
                for j in range(NG):
                    g = NG * b + j
                    ahead = first_pass(g + 1, (j + 1) % NG, b + (j + 1) // NG, last=last and j == NG - 1)
                    pe.wait_ge(v_placed[j], b + 1)
                    for n in range(BLOCKS):
                        if n % KT == 0:
                            pe.wait_ge(rows_placed[n // KT], ROWS_INC * g + (ROWS_INC + 1))
                        for h, _ in enumerate(scores(g, j, n)):
                            for _ in range(AHEAD[h] + (n % KT == 1 and h == 0)):
                                next(ahead, None)
                        if n:
                            values(g, j, n - 1)
                    values(g, j, BLOCKS - 1)

            for _ in first_pass(0, 0, 0, first=True):
                pass
            with pe.Fori(0, B - 1) as b:
                batch(b, False)
            batch(B - 1, True)


def finish_attention_phase(nc, t, dram):
    with ExitStack() as ctx:
        def sb(name, shape, dt=F32):
            return ctx.enter_context(nc.sbuf_tensor(name, shape, dt))

        def sem(name):
            return ctx.enter_context(nc.semaphore(name))

        numer = sb("numer", [P, 2, N])
        denom = sb("denom", [P, 2, N])
        inverse = sb("inverse", [P, 2, CH])
        context = sb("context", [P, 2, CH])
        gated = sb("gated", [P, 2, CH])
        squares = sb("c_squares", [P, 2, CH])
        log_var = sb("c_log_var", [P, 2, CH])
        rstd = sb("c_rstd", [P, 2, CH])
        normed = sb("c_normed", [P, 2, CH])
        ps = [ctx.enter_context(nc.psum_tensor(f"fin{i}", [P, CH], F32)) for i in range(6)]
        bank_attn, bank_c, bank_var = ps[0:2], ps[2:4], ps[4:6]
        rows_loaded = [sem(f"rows_loaded{i}") for i in range(2)]
        edge = sem("edge_cleared")
        inverted = sem("inverted")
        context_ready = sem("context_ready")
        projected = sem("projected")
        gated_ready = sem("gated_ready")
        x_updated = sem("x_updated")
        centred = sem("c_centred")
        squared = sem("c_squared")
        var_ready = sem("c_var_ready")
        log_ready = sem("c_log_ready")
        rstd_ready = sem("c_rstd_ready")
        normed_ready = sem("c_normed_ready")
        input_ready = sem("input_ready")
        block = ctx.enter_context(nc.Block())
        rows = t["head_rows"].rearrange("j (h k d) n -> k (j h) d n", h=GH, k=4)

        @block.sync
        def _(sp):
            def load(b, half):
                for k, dst in enumerate((numer, denom)):
                    sp.dma_start(dst[:, half, :], rows[k, :, :, bass.ds(b * N, N)]).then_inc(rows_loaded[half], 16)

            load(0, 0)
            load(1, 1)
            for b in range(2, B):
                sp.wait_ge(context_ready, 2 * (b - 1))
                load(b, b % 2)

        @block.gpsimd
        def _(pool):
            nc.gpsimd.memset(t["xa"][:, :, 0:1], 0.0).then_inc(edge, 1)
            nc.gpsimd.memset(t["xb"][:, :, 0:1], 0.0).then_inc(edge, 1)
            for b in range(B):
                for i in range(2):
                    n = 2 * b + i
                    pool.wait_ge(inverted, n + 1)
                    if n >= 2:
                        pool.wait_ge(projected, n - 1)
                    nc.gpsimd.tensor_tensor(context[:, i], numer[:, b % 2, i * CH:(i + 1) * CH], inverse[:, i],
                                            ALU.mult).then_inc(context_ready, 1)

        @block.scalar
        def _(act):
            nc.scalar.preload_act_table_set(TABLE_SET)
            for b in range(B):
                for i in range(2):
                    act.wait_ge(centred, 2 * b + i + 1)
                    nc.scalar.activation(squares[:, i], bank_c[i][:, :], ACT.Square).then_inc(squared, 1)
                    act.wait_ge(var_ready, 2 * b + i + 1)
                    nc.scalar.activation(log_var[:, i], bank_var[i][:, :], ACT.Ln, bias=t["eps_col"][:, :]
                                         ).then_inc(log_ready, 1)
                    act.wait_ge(log_ready, 2 * b + i + 1)
                    if b:
                        act.wait_ge(normed_ready, 2 * b + i - 1)
                    nc.scalar.activation(rstd[:, i], log_var[:, i], ACT.Exp, scale=-0.5).then_inc(rstd_ready, 1)

        @block.vector
        def _(dve):
            def invert(n):
                b, i = divmod(n, 2)
                dve.wait_ge(rows_loaded[b % 2], 32 * (b // 2) + 32)
                if n >= 2:
                    dve.wait_ge(context_ready, n - 1)
                nc.vector.reciprocal(inverse[:, i], denom[:, b % 2, i * CH:(i + 1) * CH]).then_inc(inverted, 1)

            invert(0)
            for n in range(2 * B):
                b, i = divmod(n, 2)
                if n + 1 < 2 * B:
                    invert(n + 1)
                cols = slice(n * CH, (n + 1) * CH)
                dve.wait_ge(projected, n + 1)
                nc.vector.scalar_tensor_tensor(out=gated[:, i], in0=bank_attn[i][:, :], scalar=t["mod"][:, 2, b:b + 1],
                                               in1=t["x_t"][:, cols], op0=ALU.mult, op1=ALU.add
                                               ).then_inc(gated_ready, 1)
                dve.wait_ge(gated_ready, n + 1)
                nc.vector.tensor_scalar(t["x_t"][:, cols], gated[:, i], t["ga_bias"][:, b:b + 1], None, ALU.add
                                        ).then_inc(x_updated, 1)
                dve.wait_ge(rstd_ready, n + 1)
                nc.vector.tensor_tensor(normed[:, i], bank_c[i][:, :], rstd[:, i], ALU.mult).then_inc(normed_ready, 1)
                dve.wait_ge(normed_ready, n + 1)
                nc.vector.tensor_scalar(t["xa"][:, b, 1 + i * CH:1 + (i + 1) * CH], normed[:, i],
                                        t["mod"][:, 4, b:b + 1], t["mod"][:, 3, b:b + 1], ALU.mult, ALU.add
                                        ).then_inc(input_ready, 1)

        @block.tensor
        def _(pe):
            for n in range(2 * B):
                i = n % 2
                pe.wait_ge(context_ready, n + 1)
                if n >= 2:
                    pe.wait_ge(gated_ready, n - 1)
                nc.tensor.matmul(bank_attn[i][:, :], t["wo"][:, :], context[:, i], start=True, stop=True
                                 ).then_inc(projected, 1)
                pe.wait_ge(x_updated, n + 1)
                if n >= 2:
                    pe.wait_ge(normed_ready, n - 1)
                nc.tensor.matmul(bank_c[i][:, :], t["center"][:, :], t["x_t"][:, n * CH:(n + 1) * CH],
                                 start=True, stop=True).then_inc(centred, 1)
                pe.wait_ge(squared, n + 1)
                if n >= 2:
                    pe.wait_ge(log_ready, n - 1)
                nc.tensor.matmul(bank_var[i][:, :], t["mean"][:, :], squares[:, i], start=True, stop=True
                                 ).then_inc(var_ready, 1)


def after(engine, sem, count):
    if not (isinstance(count, int) and count <= 0):
        engine.wait_ge(sem, count)


def at_most(count, last):
    return min(count, last) if isinstance(count, int) else count


def transformer_phase(nc, t, dram):
    with ExitStack() as ctx:
        def sb(name, shape, dt=F32):
            return ctx.enter_context(nc.sbuf_tensor(name, shape, dt))

        def sem(name):
            return ctx.enter_context(nc.semaphore(name))

        wqkv, wout, w1, w2, b1, b2, ln_g, ln_b, table, masks = (t[name] for name in (
            "wqkv", "wout", "w1", "w2", "b1", "b2", "ln_g", "ln_b", "table", "masks"))
        shifted = sb("shifted", [P, 2, CH])
        squares = sb("f_squares", [P, 2 * INNER])
        norms = sb("norms", [P, 2, 2 * LH])
        clipped = sb("clipped", [P, 2, 2 * LH])
        log_norm = sb("log_norm", [P, 2, 2 * LH])
        inv_norm = sb("inv_norm", [P, 2, 2 * LH])
        norm_bias = sb("norm_bias", [P, 1])
        unit = sb("unit", [P, 2, 2 * INNER])
        turn_sin = sb("turn_sin", [P, 2 * INNER])
        turned = sb("turned", [P, 2, 2 * INNER])
        q_t = sb("q_t", [P, 2, 4, P])
        k_t = sb("k_t", [P, 2, 4, P + WINDOW])
        v_aug = sb("v_aug", [P, TPB, LH, LD + 1])
        v_mix = sb("v_mix", [P, TPB, LH, LD + 1])
        top = sb("top", [P, 2, LH])
        probs = sb("f_probs", [P, 2, LH, P])
        probs_t = sb("probs_t", [P, 2, LH, P])
        inv_sum = sb("inv_sum", [P, 2, LH])
        heads = sb("heads", [P, 2, INNER])
        heads_t = sb("heads_t", [P, 4, CH])
        x_mid = sb("x_mid", [P, 2, CH + 1])
        mid_c = sb("mid_c", [P, CH])
        mid_sq = sb("mid_sq", [P, CH])
        mid_h = sb("mid_h", [P, CH])
        hidden = sb("hidden", [P, 3, CH])

        ps_qk = ctx.enter_context(nc.psum_tensor("ps_qk", [P, 2 * INNER], F32))
        ps_turn = ctx.enter_context(nc.psum_tensor("ps_turn", [P, 2 * INNER], F32))
        ps_sim = ctx.enter_context(nc.psum_tensor("ps_sim", [P, 2, 512], F32))
        ps_vo = ctx.enter_context(nc.psum_tensor("ps_vo", [P, INNER], F32))
        ps_mid = ctx.enter_context(nc.psum_tensor("ps_mid", [P, CH], F32))

        cleared = sem("f_cleared")
        qk_done = sem("qk_done")
        v_done = sem("v_done")
        turn_done = sem("turn_done")
        sim_done = sem("sim_done")
        probs_turned = sem("probs_turned")
        values_done = sem("f_values_done")
        heads_turned = sem("heads_turned")
        squared = sem("f_squared")
        normed_in = sem("normed_in")
        clipped_ready = sem("clipped_ready")
        log_ready = sem("f_log_ready")
        inv_norm_ready = sem("inv_norm_ready")
        norm_step = sem("norm_step")
        unit_ready = sem("unit_ready")
        rope_step = sem("rope_step")
        rotated = sem("rotated")
        turn_kept = sem("turn_kept")
        v_kept = sem("f_v_kept")
        top_ready = sem("top_ready")
        sim_shifted = sem("sim_shifted")
        exp_ready = sem("exp_ready")
        probs_kept = sem("probs_kept")
        inv_sum_ready = sem("inv_sum_ready")
        heads_ready = sem("heads_ready")
        heads_kept = sem("heads_kept")
        shift_ready = sem("shift_ready")
        out_projected = sem("out_projected")
        mid_ready = sem("mid_ready")
        mid_centred = sem("mid_centred")
        mid_c_kept = sem("mid_c_kept")
        mid_squared = sem("mid_squared")
        mid_var = sem("mid_var")
        mid_logged = sem("mid_logged")
        mid_rstd_ready = sem("mid_rstd_ready")
        mid_step = sem("mid_step")
        mid_normed = sem("mid_normed")
        mid_h_ready = sem("mid_h_ready")
        gate_done = sem("gate_done")
        gate_kept = sem("gate_kept")
        gelu_ready = sem("gelu_ready")
        linear_done = sem("linear_done")
        hidden_ready = sem("hidden_ready")
        down_done = sem("down_done")
        x_out = sem("x_out")
        block = ctx.enter_context(nc.Block())

        def iterate(engine, part):
            def eight(it, tile_layer, chunk_layer):
                for sigma in range(TPB):
                    part(it, sigma, tile_layer, chunk_layer)

            eight(0, 0, None)
            eight(1, 0, 0)
            with engine.Fori(2, B) as it:
                eight(it, 0, 0)
            eight(B, 1, 0)
            with engine.Fori(B + 1, 2 * B) as it:
                eight(it, 1, 1)
            eight(2 * B, None, 1)

        def tile_of(it, sigma, offset):
            n = TPB * it + (sigma - offset)
            if isinstance(n, int) and not 0 <= n < TILES:
                return None, None
            return n, (sigma - offset) % TPB

        def chunk_at(it, sigma):
            n = 2 * it + (sigma // 4 - 2)
            if isinstance(n, int) and not 0 <= n < CHUNKS:
                return None, None
            return n, sigma // 4

        OUT, CENTRE, VAR, SCALE, GATE, GELU, LINEAR, DOWN = 0, 1, 2, 3, (4, 5, 6), 7, (8, 9, 10), 11

        def position(sigma, third):
            return 3 * (sigma % 4) + third

        def tensor_slot(pe, it, sigma, tile_layer, chunk_layer):
            def late(third):
                c, par = chunk_at(it, sigma)
                if c is None:
                    return
                l, p = chunk_layer, position(sigma, third)
                if p == OUT:
                    after(pe, heads_kept, 4 * c + 4)
                    after(pe, x_out, c)
                    for k in range(4):
                        mm = nc.tensor.matmul(ps_mid[:, :], wout[:, l, k, :], heads_t[:, k, :],
                                              start=(k == 0), stop=(k == 3))
                    mm.then_inc(out_projected, 1)
                elif p == CENTRE:
                    after(pe, mid_ready, c + 1)
                    nc.tensor.matmul(ps_mid[:, :], t["center"][:, :], x_mid[:, par, 0:CH], start=True, stop=True
                                     ).then_inc(mid_centred, 1)
                elif p == VAR:
                    after(pe, mid_squared, c + 1)
                    after(pe, mid_c_kept, c + 1)
                    nc.tensor.matmul(ps_mid[:, :], t["mean"][:, :], mid_sq[:, :], start=True, stop=True
                                     ).then_inc(mid_var, 1)
                elif p in GATE:
                    k = GATE.index(p)
                    at, n = HCH[k]
                    if k == 0:
                        after(pe, mid_h_ready, c + 1)
                    else:
                        after(pe, gate_kept, 3 * c + k)
                    nc.tensor.matmul(ps_mid[0:n, :], w1[:, l, HID + at:HID + at + n], mid_h[:, :],
                                     start=True, stop=True).then_inc(gate_done, 1)
                elif p in LINEAR:
                    k = LINEAR.index(p)
                    at, n = HCH[k]
                    if k == 0:
                        after(pe, gate_kept, 3 * c + 3)
                    else:
                        after(pe, hidden_ready, 3 * c + k)
                    nc.tensor.matmul(ps_mid[0:n, :], w1[:, l, at:at + n], mid_h[:, :],
                                     start=True, stop=True).then_inc(linear_done, 1)
                elif p == DOWN:
                    after(pe, hidden_ready, 3 * c + 3)
                    for k, (at, n) in enumerate(HCH):
                        mm = nc.tensor.matmul(ps_mid[:, :], w2[0:n, l, k, :], hidden[0:n, k, :],
                                              start=(k == 0), stop=(k == 2))
                    mm.then_inc(down_done, 1)

            n, i = tile_of(it, sigma, 2)
            if n is not None:
                after(pe, rotated, n + 1)
                after(pe, probs_kept, n - 1)
                for k in range(8):
                    mm = nc.tensor.transpose(ps_turn[:, k * P:(k + 1) * P], turned[:, i % 2, k * P:(k + 1) * P],
                                             t["identity"][:, :])
                mm.then_inc(turn_done, 1)
            n, i = tile_of(it, sigma, 4)
            if n is not None:
                after(pe, heads_ready, n + 1)
                after(pe, v_kept, at_most(n + 4, TILES))
                if tile_layer is None:
                    after(pe, heads_kept, n)
                for k in range(4):
                    mm = nc.tensor.transpose(ps_vo[:, k * P:(k + 1) * P], heads[:, i % 2, k * P:(k + 1) * P],
                                             t["identity"][:, :])
                mm.then_inc(heads_turned, 1)
            late(0)
            n, i = tile_of(it, sigma, 2)
            if n is not None:
                after(pe, turn_kept, n + 1)
                after(pe, heads_ready, n - 1)
                mask = masks[:, 0 if i == 0 else 1, :]
                for bank in range(2):
                    nc.tensor.matmul(ps_sim[:, bank, :], t["identity_bf"][:, :],
                                     mask.rearrange("p (a k) -> p a k", a=1).broadcast_to((P, 4, P)),
                                     start=True, stop=False, skip_group_check=True)
                for h in range(LH):
                    rows = slice(64 * (h % 2), 64 * (h % 2) + 64)
                    for win in range(2):
                        keys = k_t[rows, i % 2, h // 2, :]
                        keys = keys.rearrange("p (a k) -> p a k", k=WINDOW)[:, 0:3:2, :] if win == 0 else keys[:, 0:P]
                        mm = nc.tensor.matmul(ps_sim[64 * win:64 * win + 64, h % 2, (h // 2) * P:(h // 2 + 1) * P],
                                              q_t[rows, i % 2, h // 2, 64 * win:64 * win + 64], keys,
                                              start=False, stop=True, skip_group_check=True)
                mm.then_inc(sim_done, 1)
            n, i = tile_of(it, sigma, 3)
            if n is not None:
                after(pe, exp_ready, n + 1)
                after(pe, turn_kept, at_most(n + 2, TILES))
                if tile_layer is None:
                    after(pe, probs_kept, n)
                for h in range(LH):
                    mm = nc.tensor.transpose(ps_turn[:, h * P:(h + 1) * P], probs[:, i % 2, h, :],
                                             t["identity"][:, :])
                mm.then_inc(probs_turned, 1)
            n, i = tile_of(it, sigma, 0)
            if n is not None:
                own = shifted[:, (i // 4) % 2, (i % 4) * P:(i % 4 + 1) * P]
                if i % 4 == 0:
                    after(pe, shift_ready, 2 * it + (i // 4 + 1))
                after(pe, unit_ready, n)
                for w in range(2):
                    mm = nc.tensor.matmul(ps_qk[:, w * INNER:(w + 1) * INNER], own,
                                          wqkv[:, tile_layer, w * INNER:(w + 1) * INNER], start=True, stop=True)
                mm.then_inc(qk_done, 1)
                after(pe, v_kept, n)
                after(pe, heads_kept, n - 3)
                nc.tensor.matmul(ps_vo[:, :], own, wqkv[:, tile_layer, 2 * INNER:], start=True, stop=True
                                 ).then_inc(v_done, 1)
            late(1)
            n, i = tile_of(it, sigma, 3)
            if n is not None:
                after(pe, probs_kept, n + 1)
                after(pe, v_kept, n + 1)
                after(pe, sim_shifted, at_most(n + 2, TILES))
                if tile_layer is None:
                    after(pe, heads_ready, n)
                for h in range(LH):
                    out = ps_sim[:, h // 4, (h % 4) * (LD + 1):(h % 4 + 1) * (LD + 1)]
                    nc.tensor.matmul(out[0:64], probs_t[:, i % 2, h, 0:64], v_mix[:, i, h, :],
                                     start=True, stop=True)
                    mm = nc.tensor.matmul(out[64:P], probs_t[:, i % 2, h, 64:P], v_aug[:, i, h, :],
                                          start=True, stop=True)
                mm.then_inc(values_done, 1)
            late(2)

        @block.tensor
        def _(pe):
            pe.wait_ge(cleared, 5)
            iterate(pe, lambda *a: tensor_slot(pe, *a))

        def scalar_slot(act, it, sigma, tile_layer, chunk_layer):
            def late(third):
                c, par = chunk_at(it, sigma)
                if c is None:
                    return
                l, p = chunk_layer, position(sigma, third)
                if p == CENTRE:
                    after(act, mid_centred, c + 1)
                    after(act, mid_normed, c)
                    nc.scalar.activation(mid_sq[:, :], ps_mid[:, :], ACT.Square).then_inc(mid_squared, 1)
                elif p == VAR:
                    after(act, mid_var, c + 1)
                    nc.scalar.activation(mid_sq[:, :], ps_mid[:, :], ACT.Ln, bias=t["eps_col"][:, :]
                                         ).then_inc(mid_logged, 1)
                    after(act, mid_logged, c + 1)
                    nc.scalar.activation(mid_sq[:, :], mid_sq[:, :], ACT.Exp, scale=-0.5
                                         ).then_inc(mid_rstd_ready, 1)
                elif p == SCALE:
                    after(act, mid_normed, c + 1)
                    after(act, linear_done, 3 * c)
                    nc.scalar.activation(mid_h[:, :], mid_c[:, :], ACT.Identity, scale=ln_g[:, l:l + 1],
                                         bias=ln_b[:, l:l + 1]).then_inc(mid_h_ready, 1)
                elif p in GATE:
                    k = GATE.index(p)
                    at, n = HCH[k]
                    after(act, gate_done, 3 * c + (k + 1))
                    if k == 0:
                        after(act, down_done, c)
                    nc.scalar.activation(hidden[0:n, k], ps_mid[0:n, :], ACT.Identity,
                                         bias=b1[0:n, l, 1, k:k + 1]).then_inc(gate_kept, 1)
                elif p == GELU:
                    n = HCH[2][1]
                    after(act, gate_kept, 3 * c + 3)
                    nc.scalar.activation(hidden[:, 0:2, :], hidden[:, 0:2, :], ACT.Gelu).then_inc(gelu_ready, 1)
                    nc.scalar.activation(hidden[0:n, 2, :], hidden[0:n, 2, :], ACT.Gelu).then_inc(gelu_ready, 1)
                    nc.scalar.preload_act_table_set(TABLE_SET)

            n, i = tile_of(it, sigma, 2)
            if n is not None:
                after(act, turn_done, n + 1)
                after(act, sim_done, n)
                src = ps_turn[:, :].rearrange("p (w a k) -> p w a k", w=2, a=4)
                nc.scalar.activation(q_t[:, i % 2], src[:, 0], ACT.Copy)
                nc.scalar.activation(k_t[:, i % 2, :, 0:P], src[:, 1], ACT.Copy)
                nc.scalar.activation(k_t[:, (i + 1) % 2, :, P:], src[:, 1, :, WINDOW:], ACT.Copy
                                     ).then_inc(turn_kept, 1)
            n, i = tile_of(it, sigma, 4)
            if n is not None:
                after(act, heads_turned, n + 1)
                if i % 4 == 0:
                    after(act, out_projected, 2 * it + (sigma - 4) // 4)
                nc.scalar.activation(heads_t[:, :, (i % 4) * P:(i % 4 + 1) * P],
                                     ps_vo[:, :].rearrange("p (a k) -> p a k", a=4), ACT.Copy
                                     ).then_inc(heads_kept, 1)
            late(0)
            n, i = tile_of(it, sigma, 3)
            if n is not None:
                after(act, probs_turned, n + 1)
                after(act, values_done, n - 1)
                nc.scalar.activation(probs_t[:, i % 2].rearrange("p h k -> p (h k)"), ps_turn[:, :], ACT.Copy
                                     ).then_inc(probs_kept, 1)
            n, i = tile_of(it, sigma, 0)
            if n is not None:
                after(act, qk_done, n + 1)
                after(act, normed_in, n)
                nc.scalar.activation(squares[:, :], ps_qk[:, :], ACT.Square).then_inc(squared, 1)
            n, i = tile_of(it, sigma, 2)
            if n is not None:
                after(act, sim_shifted, n + 1)
                flat = probs[:, i % 2].rearrange("p h k -> p (h k)")
                nc.scalar.activation(flat, flat, ACT.Exp, scale=QK_SCALE).then_inc(exp_ready, 1)
            n, i = tile_of(it, sigma, 0)
            if n is not None:
                after(act, v_done, n + 1)
                after(act, values_done, n - 6)
                src = ps_vo[:, :].rearrange("p (h d) -> p h d", h=LH)
                nc.scalar.activation(v_aug[:, i, :, 0:LD], src, ACT.Copy)
                nc.scalar.activation(v_mix[0:64, i, :, 0:LD], src[0:64], ACT.Copy)
                nc.scalar.activation(v_mix[64:P, (i + 1) % TPB, :, 0:LD], src[64:P], ACT.Copy).then_inc(v_kept, 1)
                after(act, clipped_ready, n + 1)
                nc.scalar.activation(log_norm[:, i % 2, :], clipped[:, i % 2, :], ACT.Ln,
                                     scale=float(2 ** NORM_SHIFT)).then_inc(log_ready, 1)
                after(act, log_ready, n + 1)
                after(act, unit_ready, n - 1)
                nc.scalar.activation(inv_norm[:, i % 2, :], log_norm[:, i % 2, :], ACT.Exp, scale=-0.5,
                                     bias=norm_bias[:, :]).then_inc(inv_norm_ready, 1)
            late(1)
            late(2)

        @block.scalar
        def _(act):
            nc.scalar.preload_act_table_set(TABLE_SET)
            act.wait_ge(cleared, 5)
            iterate(act, lambda *a: scalar_slot(act, *a))

        def vector_slot(dve, it, sigma, tile_layer, chunk_layer):
            b = it - 1 - B * (chunk_layer or 0)
            x_in, x_res = (t["xa"], t["xb"]) if chunk_layer == 0 else (t["xb"], t["xa"])

            def late(third):
                c, par = chunk_at(it, sigma)
                if c is None:
                    return
                l, p = chunk_layer, position(sigma, third)
                at0 = 1 + par * CH
                if p == OUT:
                    after(dve, out_projected, c + 1)
                    nc.vector.tensor_tensor(x_mid[0:64, par, 0:CH], ps_mid[0:64, :],
                                            x_in[0:64, bass.ds(b, 1), at0:at0 + CH].rearrange("p a n -> p (a n)"),
                                            ALU.add)
                    nc.vector.tensor_tensor(x_mid[64:P, par, 1:CH + 1], ps_mid[64:P, :],
                                            x_in[64:P, bass.ds(b, 1), at0:at0 + CH].rearrange("p a n -> p (a n)"),
                                            ALU.add).then_inc(mid_ready, 1)
                    if par == 0:
                        dve.wait_ge(mid_ready, c + 1)
                        nc.vector.tensor_copy(x_mid[64:P, 1, 0:1], x_mid[64:P, 0, CH:CH + 1])
                elif p == CENTRE:
                    after(dve, mid_centred, c + 1)
                    after(dve, mid_squared, c + 1)
                    after(dve, mid_h_ready, c)
                    nc.vector.tensor_copy(mid_c[:, :], ps_mid[:, :]).then_inc(mid_c_kept, 1)
                elif p == VAR:
                    after(dve, mid_rstd_ready, c + 1)
                    after(dve, linear_done, 3 * c)
                    nc.vector.scalar_tensor_tensor(out=mid_h[:, :], in0=mid_sq[:, :], scalar=-0.5, in1=mid_sq[:, :],
                                                   op0=ALU.mult, op1=ALU.mult).then_inc(mid_step, 1)
                    after(dve, mid_step, 3 * c + 1)
                    nc.vector.scalar_tensor_tensor(out=mid_h[:, :], in0=ps_mid[:, :], scalar=EPS, in1=mid_h[:, :],
                                                   op0=ALU.add, op1=ALU.mult).then_inc(mid_step, 1)
                    after(dve, mid_step, 3 * c + 2)
                    nc.vector.scalar_tensor_tensor(out=mid_sq[:, :], in0=mid_h[:, :], scalar=1.5, in1=mid_sq[:, :],
                                                   op0=ALU.add, op1=ALU.mult).then_inc(mid_step, 1)
                    after(dve, mid_step, 3 * c + 3)
                    nc.vector.tensor_tensor(mid_c[:, :], mid_c[:, :], mid_sq[:, :], ALU.mult
                                            ).then_inc(mid_normed, 1)
                elif p in LINEAR:
                    k = LINEAR.index(p)
                    at, n = HCH[k]
                    after(dve, linear_done, 3 * c + (k + 1))
                    after(dve, gelu_ready, 2 * c + 2)
                    nc.vector.scalar_tensor_tensor(out=hidden[0:n, k, :], in0=ps_mid[0:n, :],
                                                   scalar=b1[0:n, l, 0, k:k + 1], in1=hidden[0:n, k, :],
                                                   op0=ALU.add, op1=ALU.mult).then_inc(hidden_ready, 1)
                elif p == DOWN:
                    after(dve, down_done, c + 1)
                    for lo, first in ((0, 0), (64, 1)):
                        op = nc.vector.scalar_tensor_tensor(
                            out=x_res[lo:lo + 64, bass.ds(b, 1), at0:at0 + CH].rearrange("p a n -> p (a n)"),
                            in0=ps_mid[lo:lo + 64, :], scalar=b2[lo:lo + 64, l:l + 1],
                            in1=x_mid[lo:lo + 64, par, first:first + CH], op0=ALU.add, op1=ALU.add)
                    op.then_inc(x_out, 1)

            if tile_layer is not None and sigma % 4 == 0:
                c, half = 2 * it + sigma // 4, sigma // 4
                batch = it - B * tile_layer
                src = (t["xa"], t["xb"])[tile_layer]
                if tile_layer:
                    after(dve, x_out, c - (NCH - 1))
                after(dve, v_done, 4 * (c - 1))
                for lo in (0, 64):
                    first = half * CH + (lo == 0)
                    op = nc.vector.tensor_copy(shifted[lo:lo + 64, half, :],
                                               src[lo:lo + 64, bass.ds(batch, 1), first:first + CH]
                                               .rearrange("p a n -> p (a n)"))
                op.then_inc(shift_ready, 1)
            late(0)
            n, i = tile_of(it, sigma, 2)
            if n is not None:
                after(dve, sim_done, n + 1)
                sims = ps_sim[:, :, :].rearrange("p a (h k) -> p h a k", k=P)
                nc.vector.tensor_reduce(top[:, i % 2, :].rearrange("p (h a) -> p h a", a=2), sims, AX.X, ALU.max
                                        ).then_inc(top_ready, 1)
                dve.wait_ge(top_ready, n + 1)
                after(dve, probs_turned, n - 1)
                nc.vector.tensor_tensor(probs[:, i % 2].rearrange("p (h a) k -> p h a k", a=2), sims,
                                        top[:, i % 2, :].rearrange("p (h a b) -> p h a b", a=2, b=1)
                                        .broadcast_to((P, LH // 2, 2, P)), ALU.subtract).then_inc(sim_shifted, 1)
            n, i = tile_of(it, sigma, 0)
            if n is not None:
                after(dve, squared, n + 1)
                nc.vector.tensor_reduce(norms[:, i % 2, :], squares[:, :].rearrange("p (h d) -> p h d", d=LD),
                                        AX.X, ALU.add).then_inc(normed_in, 1)
                dve.wait_ge(normed_in, n + 1)
                after(dve, log_ready, n - 1)
                nc.vector.tensor_scalar(clipped[:, i % 2, :], norms[:, i % 2, :], 1e-24, None, ALU.max
                                        ).then_inc(clipped_ready, 1)
            late(1)
            if n is not None:
                after(dve, inv_norm_ready, n + 1)
                guess, step = inv_norm[:, i % 2, :], norms[:, i % 2, :]
                nc.vector.scalar_tensor_tensor(out=step, in0=guess, scalar=-0.5, in1=guess,
                                               op0=ALU.mult, op1=ALU.mult).then_inc(norm_step, 1)
                dve.wait_ge(norm_step, 3 * n + 1)
                nc.vector.tensor_tensor(step, step, clipped[:, i % 2, :], ALU.mult).then_inc(norm_step, 1)
                dve.wait_ge(norm_step, 3 * n + 2)
                nc.vector.scalar_tensor_tensor(out=guess, in0=step, scalar=1.5, in1=guess,
                                               op0=ALU.add, op1=ALU.mult).then_inc(norm_step, 1)
                dve.wait_ge(norm_step, 3 * n + 3)
                after(dve, rotated, n - 1)
                nc.vector.tensor_tensor(
                    unit[:, i % 2, :].rearrange("p (h d) -> p h d", d=LD),
                    ps_qk[:, :].rearrange("p (h d) -> p h d", d=LD),
                    guess.rearrange("p (h a) -> p h a", a=1).broadcast_to((P, 2 * LH, LD)),
                    ALU.mult).then_inc(unit_ready, 1)
            n, i = tile_of(it, sigma, 3)
            if n is not None:
                after(dve, values_done, n + 1)
                outs = ps_sim[:, :, 0:4 * (LD + 1)].rearrange("p a (h d) -> p a h d", d=LD + 1)
                nc.vector.reciprocal(inv_sum[:, i % 2, :].rearrange("p (a h d) -> p a h d", a=2, d=1),
                                     outs[:, :, :, LD:]).then_inc(inv_sum_ready, 1)
                dve.wait_ge(inv_sum_ready, n + 1)
                after(dve, heads_turned, n - 1)
                for a in range(2):
                    op = nc.vector.tensor_tensor(
                        heads[:, i % 2, a * 4 * LD:(a + 1) * 4 * LD].rearrange("p (h d) -> p h d", d=LD),
                        outs[:, a, :, 0:LD],
                        inv_sum[:, i % 2, 4 * a:4 * a + 4].rearrange("p (h d) -> p h d", d=1)
                        .broadcast_to((P, 4, LD)), ALU.mult)
                op.then_inc(heads_ready, 1)
            late(2)

        @block.vector
        def _(dve):
            nc.vector.memset(v_mix[64:P, 0, :, 0:LD], 0.0).then_inc(cleared, 1)
            nc.vector.memset(k_t[:, 0, :, P:], 0.0).then_inc(cleared, 1)
            nc.vector.memset(norm_bias[:, :], float(0.5 * NORM_SHIFT * np.log(2.0))).then_inc(cleared, 1)
            nc.vector.memset(x_mid[:, 0, 0:1], 0.0)
            nc.vector.memset(v_mix[:, :, :, LD:LD + 1], 1.0).then_inc(cleared, 1)
            nc.vector.memset(v_aug[:, :, :, LD:LD + 1], 1.0).then_inc(cleared, 1)
            iterate(dve, lambda *a: vector_slot(dve, *a))

        def gpsimd_slot(pool, it, sigma, tile_layer, chunk_layer):
            n, i = tile_of(it, sigma, 1)
            if n is not None:
                l = tile_layer if sigma and tile_layer is not None else chunk_layer
                l = 0 if l is None else l
                after(pool, unit_ready, n + 1)
                after(pool, turn_done, n - 1)
                x = unit[:, i % 2, :].rearrange("p (w h d) -> p w h d", w=2, d=LD)
                tab = lambda part: table[:, l, part, i].rearrange("p w (a d) -> p w a d", a=1)
                a_out = turned[:, i % 2, :].rearrange("p (w h d) -> p w h d", w=2, d=LD)
                b_out = turn_sin[:, :].rearrange("p (w h d) -> p w h d", w=2, d=LD)
                for w in range(2):
                    nc.gpsimd.tensor_tensor(a_out[:, w], x[:, w], tab(0)[:, w].broadcast_to((P, LH, LD)), ALU.mult
                                            ).then_inc(rope_step, 1)
                for half in range(2):
                    d, e = half * LD // 2, (1 - half) * LD // 2
                    for w in range(2):
                        nc.gpsimd.tensor_tensor(b_out[:, w, :, d:d + LD // 2], x[:, w, :, e:e + LD // 2],
                                                tab(1)[:, w, :, d:d + LD // 2].broadcast_to((P, LH, LD // 2)),
                                                ALU.mult).then_inc(rope_step, 1)
                pool.wait_ge(rope_step, 6 * n + 6)
                nc.gpsimd.tensor_tensor(turned[:, i % 2, :], turned[:, i % 2, :], turn_sin[:, :], ALU.add
                                        ).then_inc(rotated, 1)
                pool.wait_ge(rotated, n + 1)

        @block.gpsimd
        def _(pool):
            iterate(pool, lambda *a: gpsimd_slot(pool, *a))


def output_phase(nc, t, out):
    with ExitStack() as ctx:
        def sem(name):
            return ctx.enter_context(nc.semaphore(name))

        total = ctx.enter_context(nc.sbuf_tensor("total", [P, 2, CH], F32))
        rows = ctx.enter_context(nc.sbuf_tensor("rows", [P, 2, CH], F32))
        ps = [ctx.enter_context(nc.psum_tensor(f"o_turn{i}", [P, CH], F32)) for i in range(2)]
        total_ready = sem("total_ready")
        o_turned = sem("o_turned")
        o_kept = sem("o_kept")
        stored = [sem(f"stored{i}") for i in range(2)]
        block = ctx.enter_context(nc.Block())
        out_v = out.rearrange("b (t p) d -> p (b t) d", p=P)

        @block.vector
        def _(dve):
            for n in range(NCH):
                b, i = divmod(n, 2)
                if n >= 2:
                    dve.wait_ge(o_turned, n - 1)
                nc.vector.scalar_tensor_tensor(out=total[:, i], in0=t["xa"][:, b, 1 + i * CH:1 + (i + 1) * CH],
                                               scalar=t["mod"][:, 5, b:b + 1], in1=t["x_t"][:, n * CH:(n + 1) * CH],
                                               op0=ALU.mult, op1=ALU.add).then_inc(total_ready, 1)

        @block.tensor
        def _(pe):
            for n in range(NCH):
                i = n % 2
                pe.wait_ge(total_ready, n + 1)
                if n >= 2:
                    pe.wait_ge(o_kept, n - 1)
                for k in range(TPC):
                    mm = nc.tensor.transpose(ps[i][:, k * P:(k + 1) * P], total[:, i, k * P:(k + 1) * P],
                                             t["identity"][:, :])
                mm.then_inc(o_turned, 1)

        @block.scalar
        def _(act):
            for n in range(NCH):
                i = n % 2
                act.wait_ge(o_turned, n + 1)
                if n >= 2:
                    act.wait_ge(stored[i], 16 * (n // 2))
                nc.scalar.activation(rows[:, i], ps[i][:, :], ACT.Copy).then_inc(o_kept, 1)

        @block.sync
        def _(sp):
            for n in range(NCH):
                i = n % 2
                sp.wait_ge(o_kept, n + 1)
                sp.dma_start(out_v[:, n * TPC:(n + 1) * TPC, :], rows[:, i].rearrange("p (t d) -> p t d", d=D)
                             ).then_inc(stored[i], 16)
            for i in range(2):
                sp.wait_ge(stored[i], 16 * (NCH // 2))


def build(nc, dram, out):
    with ExitStack() as whole:
        t = {}

        def sb(name, shape, dt=F32, scope=whole):
            t[name] = scope.enter_context(nc.sbuf_tensor(name, shape, dt))

        sb("identity", [P, P])
        sb("identity_bf", [P, P], BF16)
        sb("center", [P, P])
        sb("mean", [P, P])
        sb("eps_col", [P, 1])
        sb("c_t", [P, B])
        sb("mod", [P, 6, B])
        sb("wo_bv", [P, 1])
        sb("ga_bias", [P, B])
        sb("bias4", [P, 4])
        sb("wo", [D, D])
        sb("x_t", [P, TOK])
        sb("wqkv", [D, DEPTH, 3 * INNER])
        sb("wout", [P, DEPTH, INNER // P, D])
        sb("w1", [D, DEPTH, 2 * HID])
        sb("w2", [P, DEPTH, 3, D])
        sb("b1", [P, DEPTH, 2, 3])
        sb("b2", [P, DEPTH])
        sb("ln_g", [P, DEPTH])
        sb("ln_b", [P, DEPTH])
        sb("table", [P, DEPTH, 2, TPB, 2, LD])
        sb("masks", [P, 2, P], BF16)
        t["part_rows"] = nc.dram_tensor("part_rows", (2, H, len(QROWS), HD, TOK), BF16, kind="Internal").ap()
        t["head_rows"] = nc.dram_tensor("head_rows", (NG, P, TOK), F32, kind="Internal").ap()
        with ExitStack() as first:
            sb("wmod", [D, 6 * D], scope=first)
            sb("wq", [D, D], scope=first)
            sb("wk", [D, D], scope=first)
            sb("wv", [D, D], scope=first)
            sb("v_all", [P, B * TPB, D], scope=first)
            sb("q_stack", [STACK, PAIRS, N], BF16, scope=first)
            sb("k_stack", [STACK, H, N], BF16, scope=first)
            t["parts_saved"] = first.enter_context(nc.semaphore("parts_saved"))
            t["stacked"] = [first.enter_context(nc.semaphore(f"stacked{j}")) for j in range(NG)]
            sb("v_slots", [P, NG, TPB, GH, VW], scope=first)
            sb("row_max", [P, 2, TPC, GH], scope=first)
            sb("max_rest", [P, 2, TPC, GH], scope=first)
            sb("zeros", [P, TPC, GH], scope=first)
            sb("max_parts", [P, 2, TPC, GH, MROWS], BF16, scope=first)
            sb("max_rows", [GH * MROWS, 2, CH], BF16, scope=first)
            with ExitStack() as parts:
                sb("qk_parts", [P, 2, 3, TOK], BF16, scope=parts)
                prep_phase(nc, t, dram)
            attention_phase(nc, t, dram)
        with ExitStack() as second:
            sb("xa", [P, B, N + 1], scope=second)
            sb("xb", [P, B, N + 1], scope=second)
            finish_attention_phase(nc, t, dram)
            transformer_phase(nc, t, dram)
            output_phase(nc, t, out)


def shape_constants():
    eye = np.eye(P, dtype=np.float32)
    half = np.arange(0, LD, 2, dtype=np.float32)
    inv_freq = (np.float32(1.0) / np.power(np.float32(10000.0), half / np.float32(LD))).astype(np.float32)
    tok = np.arange(N, dtype=np.float32)
    freqs = np.tile(tok[:, None] * inv_freq[None, :], (1, 2)).astype(np.float64)
    base = ((half + np.float32(0.4 * LD)) / np.float32(1.4 * LD)).astype(np.float64)
    power = ((tok - N // 2) / np.float32(WINDOW // 2)).astype(np.float64)
    scale = np.tile(base[None, :] ** power[:, None], (1, 2))
    sign = np.where(np.arange(LD) < LD // 2, -1.0, 1.0)
    rope = np.empty((N, 2, 2, LD), np.float64)
    for w, s in enumerate((scale, 1.0 / scale)):
        rope[:, 0, w] = np.cos(freqs) * s
        rope[:, 1, w] = np.sin(freqs) * sign * s
    rope = rope.reshape(TPB, P, 2, 2, LD).transpose(1, 2, 0, 3, 4).reshape(P, -1).astype(np.float32)

    masks = np.full((P, 2, P), -1e30, np.float32)
    a, b = np.arange(WINDOW)[:, None], np.arange(WINDOW)[None, :]
    own, before = np.where(b <= a, 0.0, -1e30), np.where(b >= a, 0.0, -1e30)
    for v in range(2):
        masks[:WINDOW, v, :WINDOW] = own
        if v:
            masks[:WINDOW, v, WINDOW:] = before
        masks[WINDOW:, v, :WINDOW] = before
        masks[WINDOW:, v, WINDOW:] = own
    return {"identity": eye, "center": eye - np.float32(1.0 / D),
            "rope": rope, "masks": masks.reshape(P, 2 * P)}


_INS = ["L0_attn_x", "L0_attn_Wq", "L0_attn_bq", "L0_attn_Wk", "L0_attn_bk", "L0_attn_Wv", "L0_attn_bv",
        "L0_attn_Wo", "L0_attn_bo", "L0_ffn_wqkv", "L0_ffn_q_scale", "L0_ffn_k_scale", "L0_ffn_wo", "L0_ffn_ln_g",
        "L0_ffn_ln_b", "L0_ffn_w1", "L0_ffn_b1", "L0_ffn_w2", "L0_ffn_b2", "L0_c", "L0_wmod"]


def kernel(**inputs):
    import concourse.bacc as _bacc
    from concourse.bass_utils import run_bass_kernel_spmd as _run

    nc = _bacc.Bacc("TRN2", target_bir_lowering=False, num_devices=1)
    arrays = {name: np.ascontiguousarray(inputs[name]) for name in _INS}
    arrays.update(shape_constants())
    dram = {name: nc.dram_tensor(f"in_{name}_dram", a.shape, mybir.dt.from_np(a.dtype), kind="ExternalInput").ap()
            for name, a in arrays.items()}
    out = nc.dram_tensor("out_0_dram", (B, N, D), F32, kind="ExternalOutput").ap()
    build(nc, dram, out)
    r = _run(nc, [{f"in_{name}_dram": a for name, a in arrays.items()}], core_ids=[0])
    return r.results[0]["out_0_dram"]
```

```python
from contextlib import ExitStack
from itertools import chain

import numpy as np

import concourse.bass as bass
from concourse import mybir

F32 = mybir.dt.float32
BF16 = mybir.dt.bfloat16
ALU = mybir.AluOpType
ACT = mybir.ActivationFunctionType
AX = mybir.AxisListType

P = 128
B, N, D = 4, 1024, 128
H, HD = 16, 8
TOK = B * N
CH = 512
NCH = TOK // CH
TPC = CH // P
TPB = N // P
GH = 4
NG = H // GH
PAIRS = H // 2
QROWS = (0, 1, 2, 0, 1, 0)
KROWS = (0, 0, 0, 1, 1, 2)
SROWS = HD * len(QROWS)
MROWS = 3
PROWS = 2 * SROWS
STACK = PROWS + 2 * MROWS
VW = 2 * HD
ATT_SCALE = float(1.0 / np.sqrt(np.float32(HD)))
EPS = 1e-5

LH, LD = 8, 64
INNER = LH * LD
WINDOW = 64
HID = 341
HCH = ((0, 128), (128, 128), (256, HID - 256))
DEPTH = 2
TILES = DEPTH * B * TPB
CHUNKS = DEPTH * NCH
QK_SCALE = 8.0
NORM_SHIFT = 16


TABLE_SET = "natural_log_exp_and_others"
SAVE_INC = 16 * 2 * len(QROWS)
FILL_INC = 16 * 4
LOW_CREDIT = 4


def fill_stack(sp, t, b, j):
    for w, (name, step) in enumerate((("q_stack", 1), ("k_stack", 2))):
        for par in range(2):
            first = 2 * j if w == 0 else GH * j + par
            src = t["part_rows"][w, :, :, :, bass.ds(b * N, N)].rearrange(
                "(p a) r d n -> a p (r d) n", a=2)[par, 2 * j:2 * j + 2].rearrange("p r n -> r p n")
            dst = t[name][SROWS * par:SROWS * (par + 1), first:first + step + 1:step, :]
            sp.dma_start(dst, src).then_inc(t["stacked"][j], 16)


def save_parts(sp, t, b):
    sp.wait_ge(t["low_ready"], LOW_CREDIT + 4 * b + 4)
    for w, rows in enumerate((QROWS, KROWS)):
        for r, part in enumerate(rows):
            sp.dma_start(t["part_rows"][w, :, r, :, bass.ds(b * N, N)],
                         t["qk_parts"][:, w, part, bass.ds(b * N, N)]).then_inc(t["parts_saved"], 16)


def prep_phase(nc, t, dram):
    with ExitStack() as ctx:
        def sb(name, shape, dt=F32):
            return ctx.enter_context(nc.sbuf_tensor(name, shape, dt))

        def sem(name):
            return ctx.enter_context(nc.semaphore(name))

        x_tok = sb("x_tok", [P, 2, TPC, D])
        rstd = sb("a_rstd", [P, 2, CH])
        h_mod = sb("a_h_mod", [P, 2, CH])
        rest = sb("a_rest", [P, 2, 2, CH])
        silu_c = sb("silu_c", [P, B])
        c_exp = sb("c_exp", [P, B])
        c_den = sb("c_den", [P, B])
        c_rec = sb("c_rec", [P, B])
        gate_sign = sb("gate_sign", [P, 2, B])
        gate_neg = sb("gate_neg", [P, 2, B])
        gate_abs = sb("gate_abs", [P, 2, B])
        banks = [ctx.enter_context(nc.psum_tensor(f"prep{i}", [P, CH], F32)) for i in range(8)]
        bank_q, bank_cv, bank_vk, bank_x = banks[0:2], banks[2:4], banks[4:6], banks[6:8]
        ps_mod = bank_q[0]

        const_loaded = sem("const_loaded")
        x_loaded = [sem(f"x_loaded{i}") for i in range(2)]
        consts_set = sem("consts_set")
        k_clear = sem("k_clear")
        silu_step = sem("silu_step")
        c_exp_ready = sem("c_exp_ready")
        mod_ready = sem("mod_ready")
        mod_step = sem("mod_step")
        bias_ready = sem("bias_ready")
        x_turned = sem("x_turned")
        x_kept = sem("x_kept")
        centred = sem("centred")
        squared = sem("squared")
        var_ready = sem("var_ready")
        log_ready = sem("log_ready")
        rstd_ready = sem("rstd_ready")
        normed_ready = sem("normed_ready")
        h_ready = sem("h_ready")
        qk_ready = sem("qk_ready")
        v_ready = sem("v_ready")
        high_ready = sem("high_ready")
        rest_ready = sem("rest_ready")
        mid_ready = sem("mid_ready")
        low_ready = t["low_ready"]
        v_kept = sem("v_kept")
        block = ctx.enter_context(nc.Block())

        x_dram = dram["L0_attn_x"].rearrange("b (t p) d -> p (b t) d", p=P)
        consts = [
            (t["wmod"][:, :], dram["L0_wmod"]),
            (t["c_t"][:, :], dram["L0_c"].rearrange("b d -> d b")),
            (t["identity"][:, :], dram["identity"]),
            (t["center"][:, :], dram["center"]),
            (t["wq"][:, :], dram["L0_attn_Wq"]),
            (t["wk"][:, :], dram["L0_attn_Wk"]),
            (t["wv"][:, :], dram["L0_attn_Wv"]),
            (t["wo"][:, :], dram["L0_attn_Wo"]),
        ] + [(t["bias4"][:, i:i + 1], dram[f"L0_attn_{n}"].rearrange("(p a) -> p a", a=1))
             for i, n in enumerate(("bq", "bk", "bv", "bo"))]

        @block.sync
        def _(sp):
            for i in range(2):
                sp.dma_start(x_tok[:, i], x_dram[:, i * TPC:(i + 1) * TPC, :]).then_inc(x_loaded[i], 16)
            for dst, src in consts:
                sp.dma_start(dst, src, allow_slow_non_contiguous=True).then_inc(const_loaded, 16)

            def next_x(b):
                for i in range(2):
                    sp.wait_ge(x_turned, 2 * b + (i - 1))
                    sp.dma_start(x_tok[:, i], x_dram[:, (2 * b + i) * TPC:(2 * b + i + 1) * TPC, :]
                                 ).then_inc(x_loaded[i], 16)

            next_x(1)
            for b in range(B - 1):
                if b + 2 < B:
                    next_x(b + 2)
                save_parts(sp, t, b)
                if b == 1:
                    sp.wait_ge(t["parts_saved"], 2 * SAVE_INC)
                    sp.wait_ge(k_clear, 4)
                    for j in range(NG):
                        fill_stack(sp, t, 0, j)

        @block.gpsimd
        def _(pool):
            pool.sem_inc(low_ready, LOW_CREDIT)
            nc.gpsimd.memset(t["mean"][:, :], 1.0 / D).then_inc(consts_set, 1)
            nc.gpsimd.memset(t["v_slots"][:, :, :, :, HD:VW], 1.0).then_inc(consts_set, 1)
            nc.gpsimd.memset(t["eps_col"][:, :], EPS).then_inc(consts_set, 1)
            k_words = t["k_stack"][:, :, :].rearrange("p h n -> p (h n)").bitcast(mybir.dt.uint32)
            nc.gpsimd.memset(k_words, 0).then_inc(k_clear, 1)
            pool.wait_ge(k_clear, 1)
            nc.gpsimd.memset(t["k_stack"][PROWS:STACK, 1::2, :], 1.0).then_inc(k_clear, 1)
            pool.wait_ge(k_clear, 2)
            nc.gpsimd.memset(t["k_stack"][PROWS:PROWS + MROWS, 1::2, :], 0.0).then_inc(k_clear, 1)
            pool.wait_ge(k_clear, 3)
            nc.gpsimd.memset(t["k_stack"][PROWS:PROWS + MROWS, 0::2, :], 1.0).then_inc(k_clear, 1)
            pool.wait_ge(k_clear, 4)
            with pool.Fori(0, B) as b:
                for i in range(2):
                    for w in range(2):
                        where = bass.ds((2 * b + i) * CH, CH)
                        mid, low = t["qk_parts"][:, w, 1, where], t["qk_parts"][:, w, 2, where]
                        pool.wait_ge(mid_ready, 4 * b + (2 * i + w + 1))
                        nc.gpsimd.tensor_tensor(low, rest[:, i, w], mid, ALU.subtract).then_inc(low_ready, 1)

        @block.scalar
        def _(act):
            nc.scalar.preload_act_table_set(TABLE_SET)
            act.wait_ge(const_loaded, 16 * len(consts))
            nc.scalar.activation(c_exp[:, :], t["c_t"][:, :], ACT.Exp, scale=-1.0).then_inc(c_exp_ready, 1)
            act.wait_ge(consts_set, 3)
            with act.Fori(0, B) as b:
                for i in range(2):
                    act.wait_ge(centred, 2 * b + (i + 1))
                    nc.scalar.activation(rstd[:, i], bank_cv[i][:, :], ACT.Square).then_inc(squared, 1)
                for i in range(2):
                    act.wait_ge(var_ready, 2 * b + (i + 1))
                    nc.scalar.activation(rstd[:, i], bank_vk[i][:, :], ACT.Ln, bias=t["eps_col"][:, :]
                                         ).then_inc(log_ready, 1)
                    act.wait_ge(log_ready, 2 * b + (i + 1))
                    nc.scalar.activation(rstd[:, i], rstd[:, i], ACT.Exp, scale=-0.5).then_inc(rstd_ready, 1)
                for i in range(2):
                    for w, bank in enumerate((bank_q[i], bank_vk[i])):
                        act.wait_ge(qk_ready, 4 * b + (2 * i + w + 1))
                        nc.scalar.activation(t["qk_parts"][:, w, 0, bass.ds((2 * b + i) * CH, CH)], bank[:, :],
                                             ACT.Identity, bias=t["bias4"][:, w:w + 1]).then_inc(high_ready, 1)
                    for w in range(2):
                        act.wait_ge(rest_ready, 4 * b + (2 * i + w + 1))
                        nc.scalar.activation(t["qk_parts"][:, w, 1, bass.ds((2 * b + i) * CH, CH)], rest[:, i, w],
                                             ACT.Copy).then_inc(mid_ready, 1)

        @block.vector
        def _(dve):
            dve.wait_ge(c_exp_ready, 1)
            nc.vector.tensor_scalar(c_den[:, :], c_exp[:, :], 1.0, None, ALU.add).then_inc(silu_step, 1)
            dve.wait_ge(silu_step, 1)
            nc.vector.reciprocal(c_rec[:, :], c_den[:, :]).then_inc(silu_step, 1)
            dve.wait_ge(silu_step, 2)
            nc.vector.tensor_tensor(silu_c[:, :], t["c_t"][:, :], c_rec[:, :], ALU.mult).then_inc(silu_step, 1)
            nc.vector.tensor_copy(t["identity_bf"][:, :], t["identity"][:, :])
            dve.wait_ge(mod_ready, 1)
            mod = t["mod"]
            nc.vector.tensor_copy(mod[:, :, :], ps_mod[:, 0:6 * B].rearrange("p (s b) -> p s b", b=B)
                                  ).then_inc(mod_step, 1)
            nc.vector.tensor_tensor(t["wo_bv"][:, :], ps_mod[:, 6 * B:6 * B + 1], t["bias4"][:, 3:4], ALU.add
                                    ).then_inc(mod_step, 1)
            dve.wait_ge(mod_step, 2)
            for s in (1, 4):
                nc.vector.tensor_scalar(mod[:, s, :], mod[:, s, :], 1.0, None, ALU.add).then_inc(mod_step, 1)
            for n, s in enumerate((2, 5)):
                nc.vector.tensor_scalar(gate_sign[:, n], mod[:, s, :], 0.0, 2.0, ALU.is_ge, ALU.mult
                                        ).then_inc(mod_step, 1)
                nc.vector.tensor_scalar(gate_neg[:, n], mod[:, s, :], -1.0, 0.25, ALU.mult, ALU.max
                                        ).then_inc(mod_step, 1)
            dve.wait_ge(mod_step, 8)
            for n, s in enumerate((2, 5)):
                nc.vector.tensor_tensor(gate_abs[:, n], mod[:, s, :], gate_neg[:, n], ALU.max).then_inc(mod_step, 1)
            dve.wait_ge(mod_step, 10)
            for n, s in enumerate((2, 5)):
                nc.vector.scalar_tensor_tensor(out=mod[:, s, :], in0=gate_sign[:, n], scalar=-1.0,
                                               in1=gate_abs[:, n], op0=ALU.add, op1=ALU.mult).then_inc(mod_step, 1)
            dve.wait_ge(mod_step, 12)
            nc.vector.tensor_scalar(t["ga_bias"][:, :], mod[:, 2, :], t["wo_bv"][:, 0:1], None, ALU.mult
                                    ).then_inc(bias_ready, 1)

            def keep_x(b):
                for i in range(2):
                    dve.wait_ge(x_turned, 2 * b + (i + 1))
                    nc.vector.tensor_copy(t["x_t"][:, bass.ds((2 * b + i) * CH, CH)], bank_x[i][:, :]
                                          ).then_inc(x_kept, 1)

            def batch(b, last):
                for i in range(2):
                    dve.wait_ge(rstd_ready, 2 * b + (i + 1))
                    nc.vector.tensor_tensor(h_mod[:, i], bank_cv[i][:, :], rstd[:, i], ALU.mult
                                            ).then_inc(normed_ready, 1)
                    dve.wait_ge(normed_ready, 2 * b + (i + 1))
                    nc.vector.tensor_scalar(h_mod[:, i], h_mod[:, i], mod[:, 1, bass.ds(b, 1)],
                                            mod[:, 0, bass.ds(b, 1)], ALU.mult, ALU.add).then_inc(h_ready, 1)
                if not last:
                    keep_x(b + 1)
                for i in range(2):
                    dve.wait_ge(v_ready, 2 * b + (i + 1))
                    nc.vector.tensor_copy(t["v_all"][:, bass.ds((2 * b + i) * TPC, TPC), :],
                                          bank_cv[i][:, :].rearrange("p (t f) -> p t f", t=TPC)).then_inc(v_kept, 1)
                    for w, bank in enumerate((bank_q[i], bank_vk[i])):
                        dve.wait_ge(high_ready, 4 * b + (2 * i + w + 1))
                        dve.wait_ge(low_ready, 4 * b + (2 * i + w + 1))
                        nc.vector.scalar_tensor_tensor(out=rest[:, i, w], in0=bank[:, :],
                                                       scalar=t["bias4"][:, w:w + 1],
                                                       in1=t["qk_parts"][:, w, 0, bass.ds((2 * b + i) * CH, CH)],
                                                       op0=ALU.add, op1=ALU.subtract).then_inc(rest_ready, 1)

            keep_x(0)
            with dve.Fori(0, B - 1) as b:
                batch(b, False)
            batch(B - 1, True)

        @block.tensor
        def _(pe):
            pe.wait_ge(const_loaded, 16 * len(consts))
            pe.wait_ge(silu_step, 3)
            for s in range(6):
                nc.tensor.matmul(ps_mod[:, s * B:(s + 1) * B], t["wmod"][:, s * D:(s + 1) * D], silu_c[:, :],
                                 start=True, stop=True)
            nc.tensor.matmul(ps_mod[:, 6 * B:6 * B + 1], t["wo"][:, :], t["bias4"][:, 2:3],
                             start=True, stop=True).then_inc(mod_ready, 1)
            pe.wait_ge(consts_set, 3)

            def turn_x(b):
                for i in range(2):
                    pe.wait_ge(x_loaded[i], 16 * b + 16)
                    for k in range(TPC):
                        mm = nc.tensor.transpose(bank_x[i][:, k * P:(k + 1) * P], x_tok[:, i, k, :],
                                                 t["identity"][:, :])
                    mm.then_inc(x_turned, 1)

            def batch(b, first=False, last=False):
                for i in range(2):
                    pe.wait_ge(x_kept, 2 * b + (i + 1))
                    if not first:
                        pe.wait_ge(v_kept, 2 * b + (i - 1))
                    nc.tensor.matmul(bank_cv[i][:, :], t["center"][:, :], t["x_t"][:, bass.ds((2 * b + i) * CH, CH)],
                                     start=True, stop=True).then_inc(centred, 1)
                for i in range(2):
                    pe.wait_ge(squared, 2 * b + (i + 1))
                    if not first:
                        pe.wait_ge(rest_ready, 4 * b + (2 * i - 2))
                    nc.tensor.matmul(bank_vk[i][:, :], t["mean"][:, :], rstd[:, i], start=True, stop=True
                                     ).then_inc(var_ready, 1)
                if not last:
                    turn_x(b + 1)
                for i in range(2):
                    pe.wait_ge(h_ready, 2 * b + (i + 1))
                    pe.wait_ge(rstd_ready, 2 * b + (i + 1))
                    for k in range(TPC):
                        mm = nc.tensor.matmul(bank_cv[i][:, k * P:(k + 1) * P], h_mod[:, i, k * P:(k + 1) * P],
                                              t["wv"][:, :], start=True, stop=True)
                    mm.then_inc(v_ready, 1)
                    nc.tensor.matmul(bank_q[i][:, :], t["wq"][:, :], h_mod[:, i], start=True, stop=True
                                     ).then_inc(qk_ready, 1)
                    nc.tensor.matmul(bank_vk[i][:, :], t["wk"][:, :], h_mod[:, i], start=True, stop=True
                                     ).then_inc(qk_ready, 1)

            turn_x(0)
            batch(0, first=True)
            with pe.Fori(1, B - 1) as b:
                batch(b)
            batch(B - 1, last=True)


def attention_phase(nc, t, dram):
    KT = N // P
    QT = CH // P
    UNITS = 2 * KT * GH
    BLOCKS = 2 * KT
    POS = QT * GH + 1
    TURN = 2
    AHEAD = (0, 3, 1, 0)
    LEAD = KT + 4
    ROWS_INC = 16 * 2
    OUT_INC = 16

    with ExitStack() as ctx:
        def sb(name, shape, dt=F32):
            return ctx.enter_context(nc.sbuf_tensor(name, shape, dt))

        def sem(name):
            return ctx.enter_context(nc.semaphore(name))

        probs = sb("probs", [P, 2, GH, CH])
        row_max, max_rest, zeros, max_parts, max_rows = (t[name] for name in (
            "row_max", "max_rest", "zeros", "max_parts", "max_rows"))
        rope = sb("rope", [P, 2, TPB, 2, LD])
        scales = sb("scales", [P, 2, 2, DEPTH, LD])
        masks_in = sb("masks_in", [P, 2 * P])
        head_out = sb("head_out", [P, 2, CH])
        ps_max = [ctx.enter_context(nc.psum_tensor(f"ps_max{i}", [P, N], F32)) for i in range(2)]
        ps_score = [ctx.enter_context(nc.psum_tensor(f"ps_score{i}", [P, CH], F32)) for i in range(2)]
        ps_out = [ctx.enter_context(nc.psum_tensor(f"ps_out{i}", [P, CH], F32)) for i in range(2)]

        loaded = sem("f_loaded")
        table_ready = sem("table_ready")
        stacked = t["stacked"]
        v_placed = [sem(f"v_placed{j}") for j in range(NG)]
        max_scores = sem("max_scores")
        max_taken = sem("max_taken")
        zeros_set = sem("zeros_set")
        part_step = sem("part_step")
        parts_ready = sem("parts_ready")
        rows_placed = [sem(f"rows_placed{c}") for c in range(2)]
        out_placed = [sem(f"out_placed{c}") for c in range(2)]
        probs_ready = sem("probs_ready")
        values_done = sem("values_done")
        out_kept = sem("out_kept")
        scores_ready = sem("scores_ready")
        block = ctx.enter_context(nc.Block())

        def positions(first, last):
            for c in range(2):
                for k in range(POS):
                    turn = k == TURN and not (first and c == 0)
                    if (k == TURN and not turn) or (last and not (turn and c == 0)):
                        continue
                    yield c, None if turn else k - (k > TURN), POS * c + k

        def taken(g, p, first=False, last=False):
            if last:
                return 2 * POS * g
            return p + 1 if first and p < TURN else 2 * POS * g + p

        def rows_turned(g, c, last=False):
            return taken(g + 1, TURN, last=last) if c else taken(g, POS + TURN)

        LOADS = [(t["wqkv"][:, :, :], dram["L0_ffn_wqkv"].rearrange("l p n -> p l n")),
                 (t["wout"][:, :, :, :].rearrange("p l c n -> p (l c) n"),
                  dram["L0_ffn_wo"].rearrange("l (c p) n -> p (l c) n", p=P)),
                 (t["w1"][:, :, :], dram["L0_ffn_w1"].rearrange("l p n -> p l n")),
                 (rope[:, :, :, :, :].rearrange("p a t w d -> p (a t w d)"), dram["rope"]),
                 (masks_in[:, :], dram["masks"]),
                 (t["b2"][:, :], dram["L0_ffn_b2"].rearrange("l p -> p l")),
                 (t["ln_g"][:, :], dram["L0_ffn_ln_g"].rearrange("l p -> p l")),
                 (t["ln_b"][:, :], dram["L0_ffn_ln_b"].rearrange("l p -> p l"))]
        for c, (at, n) in enumerate(HCH):
            LOADS.append((t["w2"][0:n, :, c], dram["L0_ffn_w2"][:, at:at + n].rearrange("l p n -> p l n")))
            for k in range(2):
                LOADS.append((t["b1"][0:n, :, k, c],
                              dram["L0_ffn_b1"][:, HID * k + at:HID * k + at + n].rearrange("l p -> p l")))
        for w, name in enumerate(("L0_ffn_q_scale", "L0_ffn_k_scale")):
            src = dram[name].rearrange("(a l) d -> a l d", a=1)
            for swapped, to, at, n in ((0, 0, 0, LD), (1, 0, LD // 2, LD // 2), (1, LD // 2, 0, LD // 2)):
                LOADS.append((scales[:, w, swapped, :, to:to + n], src[:, :, at:at + n].broadcast_to((P, DEPTH, n))))

        @block.sync
        def _(sp):
            save_parts(sp, t, B - 1)
            sp.wait_ge(t["parts_saved"], SAVE_INC * B)
            for dst, src in LOADS:
                sp.dma_start(dst, src, allow_slow_non_contiguous=True).then_inc(loaded, 16)

            def place_rows(g, j, c, last=False):
                sp.wait_ge(max_taken, rows_turned(g, c, last))
                for p in range(2):
                    sp.dma_start(t["q_stack"][PROWS:STACK, 2 * j + p, c * CH:(c + 1) * CH],
                                 max_rows[2 * MROWS * p:2 * MROWS * (p + 1), c, :]).then_inc(rows_placed[c], 16)

            def place_out(b, g, j, c):
                sp.wait_ge(out_kept, 2 * g + (c + 3))
                sp.dma_start(t["head_rows"][j, :, bass.ds(b * N + c * CH, CH)], head_out[:, c, :]
                             ).then_inc(out_placed[c], 16)

            place_rows(0, 0, 0)

            def batch(b, last):
                for j in range(NG):
                    g = NG * b + j
                    final = last and j == NG - 1
                    place_rows(g, j, 1, final)
                    if not final:
                        place_rows(g + 1, (j + 1) % NG, 0)
                    place_out(b, g, j, 0)
                    place_out(b, g, j, 1)
                    if not last:
                        sp.wait_ge(scores_ready, UNITS * g + UNITS)
                        fill_stack(sp, t, b + 1, j)

            with sp.Fori(0, B - 1) as b:
                batch(b, False)
            batch(B - 1, True)
            for c in range(2):
                sp.wait_ge(out_placed[c], OUT_INC * NG * B + 1)

        @block.gpsimd
        def _(pool):
            def place_v(b, j):
                nc.gpsimd.tensor_copy(
                    t["v_slots"][:, j, :, :, 0:HD],
                    t["v_all"][:, bass.ds(b * TPB, TPB), GH * HD * j:GH * HD * (j + 1)]
                    .rearrange("p t (h d) -> p t h d", h=GH)).then_inc(v_placed[j], 1)

            def negative_parts(g, c, first=False):
                step = 4 * (2 * g + c)
                pool.wait_ge(max_taken, taken(g, POS * (c + 1) - 1, first))
                high, mid, low = (max_parts[:, c, :, :, k] for k in range(MROWS))
                nc.gpsimd.tensor_tensor(high, zeros[:, :, :], row_max[:, c], ALU.subtract).then_inc(part_step, 1)
                pool.wait_ge(part_step, step + 1)
                nc.gpsimd.tensor_tensor(max_rest[:, c], row_max[:, c], high, ALU.add).then_inc(part_step, 1)
                pool.wait_ge(part_step, step + 2)
                nc.gpsimd.tensor_tensor(mid, zeros[:, :, :], max_rest[:, c], ALU.subtract).then_inc(part_step, 1)
                pool.wait_ge(part_step, step + 3)
                nc.gpsimd.tensor_tensor(max_rest[:, c], max_rest[:, c], mid, ALU.add).then_inc(part_step, 1)
                pool.wait_ge(part_step, step + 4)
                nc.gpsimd.tensor_tensor(low, zeros[:, :, :], max_rest[:, c], ALU.subtract).then_inc(parts_ready, 1)

            nc.gpsimd.memset(zeros[:, :, :], 0.0).then_inc(zeros_set, 1)
            pool.wait_ge(zeros_set, 1)
            for j in range(NG):
                place_v(0, j)
            for c in range(2):
                negative_parts(0, c, True)
            pool.wait_ge(loaded, 16 * len(LOADS))
            nc.gpsimd.tensor_copy(t["masks"][:, :, :].rearrange("p a k -> p (a k)"), masks_in[:, :]
                                  ).then_inc(table_ready, 1)
            for l in range(DEPTH):
                for part in range(2):
                    for w in range(2):
                        nc.gpsimd.tensor_tensor(
                            t["table"][:, l, part, :, w, :], rope[:, part, :, w, :],
                            scales[:, w, part, l:l + 1, :].broadcast_to((P, TPB, LD)), ALU.mult
                        ).then_inc(table_ready, 1)

            def batch(b, last):
                for j in range(NG):
                    g = NG * b + j
                    if not (last and j == NG - 1):
                        for c in range(2):
                            negative_parts(g + 1, c)
                    if not last:
                        pool.wait_ge(values_done, BLOCKS * g + (BLOCKS + 2))
                        place_v(b + 1, j)

            with pool.Fori(0, B - 1) as b:
                batch(b, False)
            batch(B - 1, True)

        @block.scalar
        def _(act):
            nc.scalar.preload_act_table_set(TABLE_SET)
            act.sem_inc(values_done, 2)
            for c in range(2):
                act.sem_inc(out_placed[c], 1)

            def keep_out(g, c):
                act.wait_ge(values_done, BLOCKS * g + (KT * (c + 1) + 2))
                act.wait_ge(out_placed[c], OUT_INC * g + 1)
                nc.scalar.activation(head_out[:, c], ps_out[c][:, :], ACT.Copy).then_inc(out_kept, 1)

            def batch(b):
                for j in range(NG):
                    g = NG * b + j
                    for n in range(BLOCKS):
                        act.wait_ge(values_done, BLOCKS * g + (n + 1))
                        for h in range(GH):
                            u = GH * n + h
                            act.wait_ge(scores_ready, UNITS * g + (u + 1))
                            nc.scalar.activation(probs[:, n % 2, h], ps_score[u % 2][:, :], ACT.Exp,
                                                 scale=ATT_SCALE).then_inc(probs_ready, 1)
                        if n == KT:
                            keep_out(g, 0)
                    keep_out(g, 1)

            with act.Fori(0, B - 1) as b:
                batch(b)
            batch(B - 1)

        @block.vector
        def _(dve):
            for c in range(2):
                dve.sem_inc(rows_placed[c], 1)
                nc.vector.memset(ps_out[c][:, :], 0.0).then_inc(out_kept, 1)

            def first_pass(g, first=False, last=False):
                for c, k, p in positions(first, last):
                    dve.wait_ge(max_scores, taken(g, p, first, last))
                    if k is None:
                        turned = 1 - c
                        dve.wait_ge(rows_placed[turned], ROWS_INC * (g - turned) + 1)
                        nc.vector.tensor_copy(max_rows[:, turned, :],
                                              ps_max[p % 2][0:GH * MROWS, 0:CH // 2].bitcast(BF16)
                                              ).then_inc(max_taken, 1)
                    else:
                        if k == 0 and not first:
                            dve.wait_ge(parts_ready, 2 * g + (c - 1))
                        nc.vector.tensor_reduce(row_max[:, c, k // GH, k % GH:k % GH + 1], ps_max[p % 2][:, :],
                                                AX.X, ALU.max).then_inc(max_taken, 1)

            def batch(b, last):
                for j in range(NG):
                    g = NG * b + j
                    first_pass(g + 1, last=last and j == NG - 1)

            first_pass(0, first=True)
            with dve.Fori(0, B - 1) as b:
                batch(b, False)
            batch(B - 1, True)

        @block.tensor
        def _(pe):
            pe.sem_inc(probs_ready, 2)

            def first_pass(g, j, b, begin, end, first=False, last=False):
                for c, k, p in positions(first, last):
                    if not begin <= KT * c + (TURN if k is None else k) // 2 < end:
                        continue
                    bank = ps_max[p % 2]
                    if last:
                        pe.wait_ge(max_taken, 2 * POS * g - 1)
                    elif not first or p >= 2:
                        pe.wait_ge(max_taken, taken(g, p - 2, first))
                    if k is None:
                        turned = 1 - c
                        pe.wait_ge(parts_ready, 2 * g + (turned + 1 - 2 * turned))
                        for q in range(QT):
                            mm = nc.tensor.transpose(
                                bank[0:GH * MROWS, 0:CH // 2].bitcast(BF16)[:, q * P:(q + 1) * P],
                                max_parts[:, turned, q].rearrange("p h k -> p (h k)"), t["identity_bf"][:, :])
                    else:
                        if p == 0:
                            pe.wait_ge(stacked[j], FILL_INC * b + FILL_INC)
                        q, h = c * QT + k // GH, k % GH
                        for half in range(2):
                            mm = nc.tensor.matmul(bank[:, half * CH:(half + 1) * CH],
                                                  t["q_stack"][0:PROWS, 2 * j + h // 2, q * P:(q + 1) * P],
                                                  t["k_stack"][0:PROWS, GH * j + h, half * CH:(half + 1) * CH],
                                                  start=True, stop=True)
                            if half == 0:
                                yield
                    mm.then_inc(max_scores, 1)
                    yield

            def scores(g, j, n):
                c, k = divmod(n, KT)
                for h in range(GH):
                    u = GH * n + h
                    pe.wait_ge(probs_ready, UNITS * g + (u + 1))
                    nc.tensor.matmul(ps_score[u % 2][:, :],
                                     t["k_stack"][0:STACK, GH * j + h, k * P:(k + 1) * P],
                                     t["q_stack"][0:STACK, 2 * j + h // 2, c * CH:(c + 1) * CH],
                                     start=True, stop=True).then_inc(scores_ready, 1)
                    yield

            def values(g, j, n):
                c, k = divmod(n, KT)
                pe.wait_ge(probs_ready, UNITS * g + (GH * n + GH + 2))
                if k == 0:
                    pe.wait_ge(out_kept, 2 * g + (c + 1))
                for h in range(GH):
                    mm = nc.tensor.matmul(ps_out[c][32 * h:32 * h + VW, :], t["v_slots"][:, j, k, h, :],
                                          probs[:, n % 2, h], start=(k == 0), stop=(k == KT - 1))
                mm.then_inc(values_done, 1)

            def batch(b, last):
                for j in range(NG):
                    g = NG * b + j
                    ahead = chain(first_pass(g, j, b, LEAD, BLOCKS),
                                  first_pass(g + 1, (j + 1) % NG, b + (j + 1) // NG, 0, LEAD,
                                             last=last and j == NG - 1))
                    pe.wait_ge(v_placed[j], b + 1)
                    for n in range(BLOCKS):
                        if n % KT == 0:
                            pe.wait_ge(rows_placed[n // KT], ROWS_INC * g + (ROWS_INC + 1))
                        for h, _ in enumerate(scores(g, j, n)):
                            for _ in range(AHEAD[h] + ((n + LEAD) % KT == TURN // 2 and h == 0)):
                                next(ahead, None)
                        if n:
                            values(g, j, n - 1)
                    values(g, j, BLOCKS - 1)

            for _ in first_pass(0, 0, 0, 0, LEAD, first=True):
                pass
            with pe.Fori(0, B - 1) as b:
                batch(b, False)
            batch(B - 1, True)


def finish_attention_phase(nc, t, dram):
    with ExitStack() as ctx:
        def sb(name, shape, dt=F32):
            return ctx.enter_context(nc.sbuf_tensor(name, shape, dt))

        def sem(name):
            return ctx.enter_context(nc.semaphore(name))

        numer = sb("numer", [P, 2, N])
        denom = sb("denom", [P, 2, N])
        inverse = sb("inverse", [P, 2, CH])
        inv_step = sb("inv_step", [P, 2, CH])
        context = sb("context", [P, 2, CH])
        gated = sb("gated", [P, 2, CH])
        squares = sb("c_squares", [P, 2, CH])
        rstd = sb("c_rstd", [P, 2, CH])
        normed = sb("c_normed", [P, 2, CH])
        minus_ga = sb("minus_ga", [P, B])
        ps = [ctx.enter_context(nc.psum_tensor(f"fin{i}", [P, CH], F32)) for i in range(6)]
        bank_attn, bank_c, bank_var = ps[0:2], ps[2:4], ps[4:6]
        rows_loaded = [sem(f"rows_loaded{i}") for i in range(2)]
        edge = sem("edge_cleared")
        ga_ready = sem("ga_ready")
        den_logged = sem("den_logged")
        guessed = sem("guessed")
        step_ready = sem("step_ready")
        inverted = sem("inverted")
        context_ready = sem("context_ready")
        projected = sem("projected")
        gated_ready = sem("gated_ready")
        x_updated = sem("x_updated")
        centred = sem("c_centred")
        squared = sem("c_squared")
        var_ready = sem("c_var_ready")
        log_ready = sem("c_log_ready")
        rstd_ready = sem("c_rstd_ready")
        normed_ready = sem("c_normed_ready")
        input_ready = sem("input_ready")
        block = ctx.enter_context(nc.Block())

        def slots():
            for s in range(NCH + 3):
                yield tuple(n if 0 <= n < NCH else None for n in (s, s - 2, s - 3))

        def half(n):
            return (n // 2) % 2, slice((n % 2) * CH, (n % 2 + 1) * CH)

        rows = t["head_rows"].rearrange("j (h k d) n -> k (j h) d n", h=GH, k=4)

        @block.sync
        def _(sp):
            def load(b, half):
                for k, dst in enumerate((numer, denom)):
                    sp.dma_start(dst[:, half, :], rows[k, :, :, bass.ds(b * N, N)]).then_inc(rows_loaded[half], 16)

            load(0, 0)
            load(1, 1)
            for b in range(2, B):
                sp.wait_ge(context_ready, 2 * (b - 1))
                load(b, b % 2)

        @block.gpsimd
        def _(pool):
            nc.gpsimd.memset(t["xa"][:, :, 0:1], 0.0).then_inc(edge, 1)
            nc.gpsimd.memset(t["xb"][:, :, 0:1], 0.0).then_inc(edge, 1)
            for n in range(NCH):
                pool.wait_ge(inverted, n + 1)
                if n >= 2:
                    pool.wait_ge(projected, n - 1)
                b, cols = half(n)
                nc.gpsimd.tensor_tensor(context[:, n % 2], numer[:, b, cols], inverse[:, n % 2], ALU.mult
                                        ).then_inc(context_ready, 1)

        @block.scalar
        def _(act):
            nc.scalar.preload_act_table_set(TABLE_SET)
            act.wait_ge(ga_ready, 1)
            for first, second, third in slots():
                if second is not None:
                    n, i = second, second % 2
                    act.wait_ge(projected, n + 1)
                    if n >= 2:
                        act.wait_ge(x_updated, n - 1)
                    nc.scalar.activation(gated[:, i], bank_attn[i][:, :], ACT.Identity,
                                         scale=minus_ga[:, n // 2:n // 2 + 1], bias=t["ga_bias"][:, n // 2:n // 2 + 1]
                                         ).then_inc(gated_ready, 1)
                if first is not None:
                    n, i = first, first % 2
                    b, cols = half(n)
                    act.wait_ge(rows_loaded[b], 32 * (n // 4) + 32)
                    if n >= 2:
                        act.wait_ge(context_ready, n - 1)
                    nc.scalar.activation(inverse[:, i], denom[:, b, cols], ACT.Ln).then_inc(den_logged, 1)
                    act.wait_ge(den_logged, n + 1)
                    nc.scalar.activation(inverse[:, i], inverse[:, i], ACT.Exp, scale=-1.0).then_inc(guessed, 1)
                if third is not None:
                    n, i = third, third % 2
                    act.wait_ge(var_ready, n + 1)
                    if n >= 2:
                        act.wait_ge(normed_ready, n - 1)
                    nc.scalar.activation(rstd[:, i], bank_var[i][:, :], ACT.Ln, bias=t["eps_col"][:, :]
                                         ).then_inc(log_ready, 1)
                    act.wait_ge(log_ready, n + 1)
                    nc.scalar.activation(rstd[:, i], rstd[:, i], ACT.Exp, scale=-0.5).then_inc(rstd_ready, 1)
                if second is not None:
                    n, i = second, second % 2
                    act.wait_ge(centred, n + 1)
                    if n >= 2:
                        act.wait_ge(var_ready, n - 1)
                    nc.scalar.activation(squares[:, i], bank_c[i][:, :], ACT.Square).then_inc(squared, 1)

        @block.vector
        def _(dve):
            nc.vector.tensor_scalar(minus_ga[:, :], t["mod"][:, 2, :], -1.0, None, ALU.mult).then_inc(ga_ready, 1)
            for first, second, third in slots():
                if second is not None:
                    n, i = second, second % 2
                    cols = slice(n * CH, (n + 1) * CH)
                    dve.wait_ge(gated_ready, n + 1)
                    nc.vector.tensor_tensor(t["x_t"][:, cols], t["x_t"][:, cols], gated[:, i], ALU.add
                                            ).then_inc(x_updated, 1)
                if first is not None:
                    n, i = first, first % 2
                    b, cols = half(n)
                    dve.wait_ge(guessed, n + 1)
                    nc.vector.tensor_tensor(inv_step[:, i], denom[:, b, cols], inverse[:, i], ALU.mult
                                            ).then_inc(step_ready, 1)
                    dve.wait_ge(step_ready, n + 1)
                    nc.vector.scalar_tensor_tensor(out=inverse[:, i], in0=inv_step[:, i], scalar=-2.0,
                                                   in1=inverse[:, i], op0=ALU.add, op1=ALU.mult
                                                   ).then_inc(inverted, 1)
                if third is not None:
                    n, i = third, third % 2
                    b, at = n // 2, 1 + i * CH
                    dve.wait_ge(rstd_ready, n + 1)
                    nc.vector.tensor_tensor(normed[:, i], bank_c[i][:, :], rstd[:, i], ALU.mult
                                            ).then_inc(normed_ready, 1)
                    dve.wait_ge(normed_ready, n + 1)
                    nc.vector.tensor_scalar(t["xa"][:, b, at:at + CH], normed[:, i], t["mod"][:, 4, b:b + 1],
                                            t["mod"][:, 3, b:b + 1], ALU.mult, ALU.add).then_inc(input_ready, 1)

        @block.tensor
        def _(pe):
            for _, second, third in slots():
                if second is not None:
                    n, i = second, second % 2
                    pe.wait_ge(context_ready, n + 1)
                    if n >= 2:
                        pe.wait_ge(gated_ready, n - 1)
                    nc.tensor.matmul(bank_attn[i][:, :], t["wo"][:, :], context[:, i], start=True, stop=True
                                     ).then_inc(projected, 1)
                if third is not None:
                    n, i = third, third % 2
                    pe.wait_ge(squared, n + 1)
                    if n >= 2:
                        pe.wait_ge(log_ready, n - 1)
                    nc.tensor.matmul(bank_var[i][:, :], t["mean"][:, :], squares[:, i], start=True, stop=True
                                     ).then_inc(var_ready, 1)
                if second is not None:
                    n, i = second, second % 2
                    pe.wait_ge(x_updated, n + 1)
                    if n >= 2:
                        pe.wait_ge(normed_ready, n - 1)
                    nc.tensor.matmul(bank_c[i][:, :], t["center"][:, :], t["x_t"][:, n * CH:(n + 1) * CH],
                                     start=True, stop=True).then_inc(centred, 1)


def after(engine, sem, count):
    if not (isinstance(count, int) and count <= 0):
        engine.wait_ge(sem, count)


def at_most(count, last):
    return min(count, last) if isinstance(count, int) else count


def transformer_phase(nc, t, out):
    with ExitStack() as ctx:
        def sb(name, shape, dt=F32):
            return ctx.enter_context(nc.sbuf_tensor(name, shape, dt))

        def sem(name):
            return ctx.enter_context(nc.semaphore(name))

        wqkv, wout, w1, w2, b1, b2, ln_g, ln_b, table, masks = (t[name] for name in (
            "wqkv", "wout", "w1", "w2", "b1", "b2", "ln_g", "ln_b", "table", "masks"))
        shifted = sb("shifted", [P, 2, CH])
        squares = sb("f_squares", [P, 2 * INNER])
        norms = sb("norms", [P, 2, 2 * LH])
        clipped = sb("clipped", [P, 2, 2 * LH])
        log_norm = sb("log_norm", [P, 2, 2 * LH])
        inv_norm = sb("inv_norm", [P, 2, 2 * LH])
        norm_bias = sb("norm_bias", [P, 1])
        unit = sb("unit", [P, 2, 2 * INNER])
        turn_sin = sb("turn_sin", [P, 2 * INNER])
        turned = sb("turned", [P, 2, 2 * INNER])
        q_t = sb("q_t", [P, 2, 4, P])
        k_t = sb("k_t", [P, 2, 4, P + WINDOW])
        v_aug = sb("v_aug", [P, TPB, LH, LD + 1])
        v_mix = sb("v_mix", [P, TPB, LH, LD + 1])
        top = sb("top", [P, 2, LH])
        probs = sb("f_probs", [P, 2, LH, P])
        probs_t = sb("probs_t", [P, 2, LH, P])
        inv_sum = sb("inv_sum", [P, 2, LH])
        heads = sb("heads", [P, 2, INNER])
        heads_t = sb("heads_t", [P, 4, CH])
        x_mid = sb("x_mid", [P, 2, CH + 1])
        mid_c = sb("mid_c", [P, CH])
        mid_sq = sb("mid_sq", [P, CH])
        mid_h = sb("mid_h", [P, CH])
        hidden = sb("hidden", [P, 3, CH])

        ps_qk = ctx.enter_context(nc.psum_tensor("ps_qk", [P, 2 * INNER], F32))
        ps_turn = ctx.enter_context(nc.psum_tensor("ps_turn", [P, 2 * INNER], F32))
        ps_sim = ctx.enter_context(nc.psum_tensor("ps_sim", [P, 2, 512], F32))
        ps_vo = ctx.enter_context(nc.psum_tensor("ps_vo", [P, INNER], F32))
        ps_mid = ctx.enter_context(nc.psum_tensor("ps_mid", [P, CH], F32))

        cleared = sem("f_cleared")
        qk_done = sem("qk_done")
        v_done = sem("v_done")
        turn_done = sem("turn_done")
        sim_done = sem("sim_done")
        probs_turned = sem("probs_turned")
        values_done = sem("f_values_done")
        heads_turned = sem("heads_turned")
        squared = sem("f_squared")
        normed_in = sem("normed_in")
        clipped_ready = sem("clipped_ready")
        log_ready = sem("f_log_ready")
        inv_norm_ready = sem("inv_norm_ready")
        norm_step = sem("norm_step")
        unit_ready = sem("unit_ready")
        rope_step = sem("rope_step")
        rotated = sem("rotated")
        turn_kept = sem("turn_kept")
        v_kept = sem("f_v_kept")
        top_ready = sem("top_ready")
        sim_shifted = sem("sim_shifted")
        exp_ready = sem("exp_ready")
        probs_kept = sem("probs_kept")
        inv_sum_ready = sem("inv_sum_ready")
        heads_ready = sem("heads_ready")
        heads_kept = sem("heads_kept")
        shift_ready = sem("shift_ready")
        out_projected = sem("out_projected")
        mid_ready = sem("mid_ready")
        mid_centred = sem("mid_centred")
        mid_c_kept = sem("mid_c_kept")
        mid_squared = sem("mid_squared")
        mid_var = sem("mid_var")
        mid_logged = sem("mid_logged")
        mid_rstd_ready = sem("mid_rstd_ready")
        mid_step = sem("mid_step")
        mid_normed = sem("mid_normed")
        mid_h_ready = sem("mid_h_ready")
        gate_done = sem("gate_done")
        gate_kept = sem("gate_kept")
        gelu_ready = sem("gelu_ready")
        linear_done = sem("linear_done")
        hidden_ready = sem("hidden_ready")
        down_done = sem("down_done")
        x_out = sem("x_out")
        total_ready = sem("total_ready")
        o_turned = sem("o_turned")
        o_kept = sem("o_kept")
        stored = [sem(f"stored{i}") for i in range(2)]
        block = ctx.enter_context(nc.Block())

        def iterate(engine, part):
            def eight(it, tile_layer, chunk_layer):
                for sigma in range(TPB):
                    part(it, sigma, tile_layer, chunk_layer)

            eight(0, 0, None)
            eight(1, 0, 0)
            with engine.Fori(2, B) as it:
                eight(it, 0, 0)
            eight(B, 1, 0)
            with engine.Fori(B + 1, 2 * B) as it:
                eight(it, 1, 1)
            eight(2 * B, None, 1)

        def tile_of(it, sigma, offset):
            n = TPB * it + (sigma - offset)
            if isinstance(n, int) and not 0 <= n < TILES:
                return None, None
            return n, (sigma - offset) % TPB

        def chunk_at(it, sigma):
            n = 2 * it + (sigma // 4 - 2)
            if isinstance(n, int) and not 0 <= n < CHUNKS:
                return None, None
            return n, sigma // 4

        OUT, CENTRE, VAR, SCALE, GATE, GELU, LINEAR, DOWN = 0, 1, 2, 4, (5, 6, 7), 8, (10, 12, 13), 14

        def position(sigma, quarter):
            return 4 * (sigma % 4) + quarter

        totals = squares[:, :].rearrange("p (i n) -> p i n", i=2)
        rows = unit[:, 0, :].rearrange("p (i n) -> p i n", i=2)
        ps_rows = ps_qk[:, :].rearrange("p (i n) -> p i n", i=2)
        out_v = out.rearrange("b (t p) d -> p (b t) d", p=P)

        def add_gated(dve, m):
            b, i = divmod(m, 2)
            dve.wait_ge(x_out, NCH + m + 1)
            if m >= 2:
                dve.wait_ge(o_turned, m - 1)
            nc.vector.scalar_tensor_tensor(out=totals[:, i], in0=t["xa"][:, b, 1 + i * CH:1 + (i + 1) * CH],
                                           scalar=t["mod"][:, 5, b:b + 1], in1=t["x_t"][:, m * CH:(m + 1) * CH],
                                           op0=ALU.mult, op1=ALU.add).then_inc(total_ready, 1)

        def turn_rows(pe, m):
            pe.wait_ge(total_ready, m + 1)
            if m == 0:
                pe.wait_ge(unit_ready, TILES)
            if m >= 2:
                pe.wait_ge(o_kept, m - 1)
            for k in range(TPC):
                mm = nc.tensor.transpose(ps_rows[:, m % 2, k * P:(k + 1) * P], totals[:, m % 2, k * P:(k + 1) * P],
                                         t["identity"][:, :])
            mm.then_inc(o_turned, 1)

        def keep_rows(act, m):
            act.wait_ge(o_turned, m + 1)
            if m == 0:
                act.wait_ge(rotated, TILES)
            if m >= 2:
                act.wait_ge(stored[m % 2], 16 * (m // 2))
            nc.scalar.activation(rows[:, m % 2], ps_rows[:, m % 2], ACT.Copy).then_inc(o_kept, 1)

        @block.sync
        def _(sp):
            for m in range(NCH):
                sp.wait_ge(o_kept, m + 1)
                sp.dma_start(out_v[:, m * TPC:(m + 1) * TPC, :], rows[:, m % 2].rearrange("p (t d) -> p t d", d=D)
                             ).then_inc(stored[m % 2], 16)
            for i in range(2):
                sp.wait_ge(stored[i], 16 * (NCH // 2))

        def tensor_slot(pe, it, sigma, tile_layer, chunk_layer):
            def late(quarter):
                c, par = chunk_at(it, sigma)
                if c is None:
                    return
                l, p = chunk_layer, position(sigma, quarter)
                if p == OUT:
                    after(pe, heads_kept, 4 * c + 4)
                    after(pe, x_out, c)
                    for k in range(4):
                        mm = nc.tensor.matmul(ps_mid[:, :], wout[:, l, k, :], heads_t[:, k, :],
                                              start=(k == 0), stop=(k == 3))
                    mm.then_inc(out_projected, 1)
                elif p == CENTRE:
                    after(pe, mid_ready, c + 1)
                    nc.tensor.matmul(ps_mid[:, :], t["center"][:, :], x_mid[:, par, 0:CH], start=True, stop=True
                                     ).then_inc(mid_centred, 1)
                elif p == VAR:
                    after(pe, mid_squared, c + 1)
                    after(pe, mid_c_kept, c + 1)
                    nc.tensor.matmul(ps_mid[:, :], t["mean"][:, :], mid_sq[:, :], start=True, stop=True
                                     ).then_inc(mid_var, 1)
                elif p in GATE:
                    k = GATE.index(p)
                    at, n = HCH[k]
                    if k == 0:
                        after(pe, mid_h_ready, c + 1)
                    else:
                        after(pe, gate_kept, 3 * c + k)
                    nc.tensor.matmul(ps_mid[0:n, :], w1[:, l, HID + at:HID + at + n], mid_h[:, :],
                                     start=True, stop=True).then_inc(gate_done, 1)
                elif p in LINEAR:
                    k = LINEAR.index(p)
                    at, n = HCH[k]
                    if k == 0:
                        after(pe, gate_kept, 3 * c + 3)
                    else:
                        after(pe, hidden_ready, 3 * c + k)
                    nc.tensor.matmul(ps_mid[0:n, :], w1[:, l, at:at + n], mid_h[:, :],
                                     start=True, stop=True).then_inc(linear_done, 1)
                elif p == DOWN:
                    after(pe, hidden_ready, 3 * c + 3)
                    for k, (at, n) in enumerate(HCH):
                        mm = nc.tensor.matmul(ps_mid[:, :], w2[0:n, l, k, :], hidden[0:n, k, :],
                                              start=(k == 0), stop=(k == 2))
                    mm.then_inc(down_done, 1)

            n, i = tile_of(it, sigma, 2)
            if n is not None:
                after(pe, rotated, n + 1)
                after(pe, probs_kept, n - 1)
                for k in range(8):
                    mm = nc.tensor.transpose(ps_turn[:, k * P:(k + 1) * P], turned[:, i % 2, k * P:(k + 1) * P],
                                             t["identity"][:, :])
                mm.then_inc(turn_done, 1)
            late(0)
            n, i = tile_of(it, sigma, 0)
            if n is not None:
                own = shifted[:, (i // 4) % 2, (i % 4) * P:(i % 4 + 1) * P]
                if i % 4 == 0:
                    after(pe, shift_ready, 2 * it + (i // 4 + 1))
                after(pe, v_kept, n)
                after(pe, heads_kept, n - 4)
                nc.tensor.matmul(ps_vo[:, :], own, wqkv[:, tile_layer, 2 * INNER:], start=True, stop=True
                                 ).then_inc(v_done, 1)
            n, i = tile_of(it, sigma, 2)
            if n is not None:
                after(pe, turn_kept, n + 1)
                after(pe, heads_ready, n - 1)
                mask = masks[:, 0 if i == 0 else 1, :]
                for bank in range(2):
                    nc.tensor.matmul(ps_sim[:, bank, :], t["identity_bf"][:, :],
                                     mask.rearrange("p (a k) -> p a k", a=1).broadcast_to((P, 4, P)),
                                     start=True, stop=False, skip_group_check=True)
                for h in range(LH):
                    rows = slice(64 * (h % 2), 64 * (h % 2) + 64)
                    for win in range(2):
                        keys = k_t[rows, i % 2, h // 2, :]
                        keys = keys.rearrange("p (a k) -> p a k", k=WINDOW)[:, 0:3:2, :] if win == 0 else keys[:, 0:P]
                        mm = nc.tensor.matmul(ps_sim[64 * win:64 * win + 64, h % 2, (h // 2) * P:(h // 2 + 1) * P],
                                              q_t[rows, i % 2, h // 2, 64 * win:64 * win + 64], keys,
                                              start=False, stop=True, skip_group_check=True)
                mm.then_inc(sim_done, 1)
            n, i = tile_of(it, sigma, 3)
            if n is not None:
                after(pe, exp_ready, n + 1)
                after(pe, turn_kept, at_most(n + 2, TILES))
                if tile_layer is None:
                    after(pe, probs_kept, n)
                for h in range(LH):
                    mm = nc.tensor.transpose(ps_turn[:, h * P:(h + 1) * P], probs[:, i % 2, h, :],
                                             t["identity"][:, :])
                mm.then_inc(probs_turned, 1)
            late(1)
            n, i = tile_of(it, sigma, 4)
            if n is not None:
                after(pe, heads_ready, n + 1)
                after(pe, v_kept, at_most(n + 5, TILES))
                if tile_layer is None:
                    after(pe, heads_kept, n)
                for k in range(4):
                    mm = nc.tensor.transpose(ps_vo[:, k * P:(k + 1) * P], heads[:, i % 2, k * P:(k + 1) * P],
                                             t["identity"][:, :])
                mm.then_inc(heads_turned, 1)
            n, i = tile_of(it, sigma, 0)
            if n is not None:
                own = shifted[:, (i // 4) % 2, (i % 4) * P:(i % 4 + 1) * P]
                after(pe, unit_ready, n)
                for w in range(2):
                    mm = nc.tensor.matmul(ps_qk[:, w * INNER:(w + 1) * INNER], own,
                                          wqkv[:, tile_layer, w * INNER:(w + 1) * INNER], start=True, stop=True)
                mm.then_inc(qk_done, 1)
            late(2)
            n, i = tile_of(it, sigma, 3)
            if n is not None:
                after(pe, probs_kept, n + 1)
                after(pe, v_kept, n + 1)
                after(pe, sim_shifted, at_most(n + 2, TILES))
                if tile_layer is None:
                    after(pe, heads_ready, n)
                for h in range(LH):
                    out = ps_sim[:, h // 4, (h % 4) * (LD + 1):(h % 4 + 1) * (LD + 1)]
                    nc.tensor.matmul(out[0:64], probs_t[:, i % 2, h, 0:64], v_mix[:, i, h, :],
                                     start=True, stop=True)
                    mm = nc.tensor.matmul(out[64:P], probs_t[:, i % 2, h, 64:P], v_aug[:, i, h, :],
                                          start=True, stop=True)
                mm.then_inc(values_done, 1)
            late(3)
            if tile_layer is None and sigma >= 2:
                turn_rows(pe, sigma - 2)

        @block.tensor
        def _(pe):
            pe.wait_ge(cleared, 5)
            iterate(pe, lambda *a: tensor_slot(pe, *a))
            for m in range(NCH - 2, NCH):
                turn_rows(pe, m)

        def scalar_slot(act, it, sigma, tile_layer, chunk_layer):
            def late(quarter):
                c, par = chunk_at(it, sigma)
                if c is None:
                    return
                l, p = chunk_layer, position(sigma, quarter)
                if p == CENTRE:
                    after(act, mid_centred, c + 1)
                    after(act, mid_normed, c)
                    nc.scalar.activation(mid_sq[:, :], ps_mid[:, :], ACT.Square).then_inc(mid_squared, 1)
                elif p == VAR:
                    after(act, mid_var, c + 1)
                    nc.scalar.activation(mid_sq[:, :], ps_mid[:, :], ACT.Ln, bias=t["eps_col"][:, :]
                                         ).then_inc(mid_logged, 1)
                    after(act, mid_logged, c + 1)
                    nc.scalar.activation(mid_sq[:, :], mid_sq[:, :], ACT.Exp, scale=-0.5
                                         ).then_inc(mid_rstd_ready, 1)
                elif p == SCALE:
                    after(act, mid_normed, c + 1)
                    after(act, linear_done, 3 * c)
                    nc.scalar.activation(mid_h[:, :], mid_c[:, :], ACT.Identity, scale=ln_g[:, l:l + 1],
                                         bias=ln_b[:, l:l + 1]).then_inc(mid_h_ready, 1)
                elif p in GATE:
                    k = GATE.index(p)
                    at, n = HCH[k]
                    after(act, gate_done, 3 * c + (k + 1))
                    if k == 0:
                        after(act, down_done, c)
                    nc.scalar.activation(hidden[0:n, k], ps_mid[0:n, :], ACT.Identity,
                                         bias=b1[0:n, l, 1, k:k + 1]).then_inc(gate_kept, 1)

            def gelu():
                c, _ = chunk_at(it, sigma)
                if c is not None and position(sigma, 0) == GELU:
                    n = HCH[2][1]
                    after(act, gate_kept, 3 * c + 3)
                    nc.scalar.activation(hidden[:, 0:2, :], hidden[:, 0:2, :], ACT.Gelu).then_inc(gelu_ready, 1)
                    nc.scalar.activation(hidden[0:n, 2, :], hidden[0:n, 2, :], ACT.Gelu).then_inc(gelu_ready, 1)
                    nc.scalar.preload_act_table_set(TABLE_SET)

            n, i = tile_of(it, sigma, 2)
            if n is not None:
                after(act, turn_done, n + 1)
                after(act, sim_done, n)
                src = ps_turn[:, :].rearrange("p (w a k) -> p w a k", w=2, a=4)
                nc.scalar.activation(q_t[:, i % 2], src[:, 0], ACT.Copy)
                nc.scalar.activation(k_t[:, i % 2, :, 0:P], src[:, 1], ACT.Copy).then_inc(turn_kept, 1)
            n, i = tile_of(it, sigma, 1)
            if n is not None:
                after(act, clipped_ready, n + 1)
                nc.scalar.activation(log_norm[:, i % 2, :], clipped[:, i % 2, :], ACT.Ln,
                                     scale=float(2 ** NORM_SHIFT)).then_inc(log_ready, 1)
                after(act, log_ready, n + 1)
                after(act, unit_ready, n - 1)
                nc.scalar.activation(inv_norm[:, i % 2, :], log_norm[:, i % 2, :], ACT.Exp, scale=-0.5,
                                     bias=norm_bias[:, :]).then_inc(inv_norm_ready, 1)
            late(0)
            n, i = tile_of(it, sigma, 0)
            if n is not None:
                after(act, v_done, n + 1)
                after(act, values_done, n - 6)
                src = ps_vo[:, :].rearrange("p (h d) -> p h d", h=LH)
                nc.scalar.activation(v_aug[:, i, :, 0:LD], src, ACT.Copy)
                nc.scalar.activation(v_mix[0:64, i, :, 0:LD], src[0:64], ACT.Copy)
                nc.scalar.activation(v_mix[64:P, (i + 1) % TPB, :, 0:LD], src[64:P], ACT.Copy).then_inc(v_kept, 1)
            n, i = tile_of(it, sigma, 2)
            if n is not None:
                after(act, turn_kept, n + 1)
                nc.scalar.activation(k_t[:, (i + 1) % 2, :, P:], k_t[:, i % 2, :, WINDOW:P], ACT.Copy)
            gelu()
            n, i = tile_of(it, sigma, 3)
            if n is not None:
                after(act, probs_turned, n + 1)
                after(act, values_done, n - 1)
                nc.scalar.activation(probs_t[:, i % 2].rearrange("p h k -> p (h k)"), ps_turn[:, :], ACT.Copy
                                     ).then_inc(probs_kept, 1)
            late(1)
            n, i = tile_of(it, sigma, 4)
            if n is not None:
                after(act, heads_turned, n + 1)
                if i % 4 == 0:
                    after(act, out_projected, 2 * it + (sigma - 4) // 4)
                nc.scalar.activation(heads_t[:, :, (i % 4) * P:(i % 4 + 1) * P],
                                     ps_vo[:, :].rearrange("p (a k) -> p a k", a=4), ACT.Copy
                                     ).then_inc(heads_kept, 1)
            n, i = tile_of(it, sigma, 0)
            if n is not None:
                after(act, qk_done, n + 1)
                after(act, normed_in, n)
                nc.scalar.activation(squares[:, :], ps_qk[:, :], ACT.Square).then_inc(squared, 1)
            late(2)
            n, i = tile_of(it, sigma, 2)
            if n is not None:
                after(act, sim_shifted, n + 1)
                flat = probs[:, i % 2].rearrange("p h k -> p (h k)")
                nc.scalar.activation(flat, flat, ACT.Exp, scale=QK_SCALE).then_inc(exp_ready, 1)
            late(3)
            if tile_layer is None and sigma >= 2:
                keep_rows(act, sigma - 2)

        @block.scalar
        def _(act):
            nc.scalar.preload_act_table_set(TABLE_SET)
            act.wait_ge(cleared, 5)
            iterate(act, lambda *a: scalar_slot(act, *a))
            for m in range(NCH - 2, NCH):
                keep_rows(act, m)

        def vector_slot(dve, it, sigma, tile_layer, chunk_layer):
            b = it - 1 - B * (chunk_layer or 0)
            x_in, x_res = (t["xa"], t["xb"]) if chunk_layer == 0 else (t["xb"], t["xa"])

            def late(quarter):
                c, par = chunk_at(it, sigma)
                if c is None:
                    return
                l, p = chunk_layer, position(sigma, quarter)
                at0 = 1 + par * CH
                if p == OUT:
                    after(dve, out_projected, c + 1)
                    nc.vector.tensor_tensor(x_mid[0:64, par, 0:CH], ps_mid[0:64, :],
                                            x_in[0:64, bass.ds(b, 1), at0:at0 + CH].rearrange("p a n -> p (a n)"),
                                            ALU.add)
                    nc.vector.tensor_tensor(x_mid[64:P, par, 1:CH + 1], ps_mid[64:P, :],
                                            x_in[64:P, bass.ds(b, 1), at0:at0 + CH].rearrange("p a n -> p (a n)"),
                                            ALU.add).then_inc(mid_ready, 1)
                    if par == 0:
                        dve.wait_ge(mid_ready, c + 1)
                        nc.vector.tensor_copy(x_mid[64:P, 1, 0:1], x_mid[64:P, 0, CH:CH + 1])
                elif p == CENTRE:
                    after(dve, mid_centred, c + 1)
                    after(dve, mid_squared, c + 1)
                    after(dve, mid_h_ready, c)
                    nc.vector.tensor_copy(mid_c[:, :], ps_mid[:, :]).then_inc(mid_c_kept, 1)
                elif p == VAR:
                    after(dve, mid_rstd_ready, c + 1)
                    after(dve, linear_done, 3 * c)
                    nc.vector.scalar_tensor_tensor(out=mid_h[:, :], in0=mid_sq[:, :], scalar=-0.5, in1=mid_sq[:, :],
                                                   op0=ALU.mult, op1=ALU.mult).then_inc(mid_step, 1)
                    after(dve, mid_step, 3 * c + 1)
                    nc.vector.scalar_tensor_tensor(out=mid_h[:, :], in0=ps_mid[:, :], scalar=EPS, in1=mid_h[:, :],
                                                   op0=ALU.add, op1=ALU.mult).then_inc(mid_step, 1)
                    after(dve, mid_step, 3 * c + 2)
                    nc.vector.scalar_tensor_tensor(out=mid_sq[:, :], in0=mid_h[:, :], scalar=1.5, in1=mid_sq[:, :],
                                                   op0=ALU.add, op1=ALU.mult).then_inc(mid_step, 1)
                    after(dve, mid_step, 3 * c + 3)
                    nc.vector.tensor_tensor(mid_c[:, :], mid_c[:, :], mid_sq[:, :], ALU.mult
                                            ).then_inc(mid_normed, 1)
                elif p in LINEAR:
                    k = LINEAR.index(p)
                    at, n = HCH[k]
                    after(dve, linear_done, 3 * c + (k + 1))
                    after(dve, gelu_ready, 2 * c + 2)
                    nc.vector.scalar_tensor_tensor(out=hidden[0:n, k, :], in0=ps_mid[0:n, :],
                                                   scalar=b1[0:n, l, 0, k:k + 1], in1=hidden[0:n, k, :],
                                                   op0=ALU.add, op1=ALU.mult).then_inc(hidden_ready, 1)
                elif p == DOWN:
                    after(dve, down_done, c + 1)
                    for lo, first in ((0, 0), (64, 1)):
                        op = nc.vector.scalar_tensor_tensor(
                            out=x_res[lo:lo + 64, bass.ds(b, 1), at0:at0 + CH].rearrange("p a n -> p (a n)"),
                            in0=ps_mid[lo:lo + 64, :], scalar=b2[lo:lo + 64, l:l + 1],
                            in1=x_mid[lo:lo + 64, par, first:first + CH], op0=ALU.add, op1=ALU.add)
                    op.then_inc(x_out, 1)

            if tile_layer is not None and sigma % 4 == 0:
                c, half = 2 * it + sigma // 4, sigma // 4
                batch = it - B * tile_layer
                src = (t["xa"], t["xb"])[tile_layer]
                if tile_layer:
                    after(dve, x_out, c - (NCH - 1))
                after(dve, qk_done, 4 * (c - 1))
                for lo in (0, 64):
                    first = half * CH + (lo == 0)
                    op = nc.vector.tensor_copy(shifted[lo:lo + 64, half, :],
                                               src[lo:lo + 64, bass.ds(batch, 1), first:first + CH]
                                               .rearrange("p a n -> p (a n)"))
                op.then_inc(shift_ready, 1)
            n, i = tile_of(it, sigma, 1)
            if n is not None:
                after(dve, inv_norm_ready, n + 1)
                guess, step = inv_norm[:, i % 2, :], norms[:, i % 2, :]
                nc.vector.scalar_tensor_tensor(out=step, in0=guess, scalar=-0.5, in1=guess,
                                               op0=ALU.mult, op1=ALU.mult).then_inc(norm_step, 1)
                dve.wait_ge(norm_step, 3 * n + 1)
                nc.vector.tensor_tensor(step, step, clipped[:, i % 2, :], ALU.mult).then_inc(norm_step, 1)
                dve.wait_ge(norm_step, 3 * n + 2)
                nc.vector.scalar_tensor_tensor(out=guess, in0=step, scalar=1.5, in1=guess,
                                               op0=ALU.add, op1=ALU.mult).then_inc(norm_step, 1)
                dve.wait_ge(norm_step, 3 * n + 3)
                after(dve, rotated, n - 1)
                nc.vector.tensor_tensor(
                    unit[:, i % 2, :].rearrange("p (h d) -> p h d", d=LD),
                    ps_qk[:, :].rearrange("p (h d) -> p h d", d=LD),
                    guess.rearrange("p (h a) -> p h a", a=1).broadcast_to((P, 2 * LH, LD)),
                    ALU.mult).then_inc(unit_ready, 1)
            late(0)
            n, i = tile_of(it, sigma, 2)
            if n is not None:
                after(dve, sim_done, n + 1)
                sims = ps_sim[:, :, :].rearrange("p a (h k) -> p h a k", k=P)
                nc.vector.tensor_reduce(top[:, i % 2, :].rearrange("p (h a) -> p h a", a=2), sims, AX.X, ALU.max
                                        ).then_inc(top_ready, 1)
                dve.wait_ge(top_ready, n + 1)
                after(dve, probs_turned, n - 1)
                nc.vector.tensor_tensor(probs[:, i % 2].rearrange("p (h a) k -> p h a k", a=2), sims,
                                        top[:, i % 2, :].rearrange("p (h a b) -> p h a b", a=2, b=1)
                                        .broadcast_to((P, LH // 2, 2, P)), ALU.subtract).then_inc(sim_shifted, 1)
            late(1)
            n, i = tile_of(it, sigma, 1)
            if n is not None:
                after(dve, rope_step, 6 * n + 6)
                nc.vector.tensor_tensor(turned[:, i % 2, :], turned[:, i % 2, :], turn_sin[:, :], ALU.add
                                        ).then_inc(rotated, 1)
            if position(sigma, 2) != VAR:
                late(2)
            n, i = tile_of(it, sigma, 0)
            if n is not None:
                after(dve, squared, n + 1)
                nc.vector.tensor_reduce(norms[:, i % 2, :], squares[:, :].rearrange("p (h d) -> p h d", d=LD),
                                        AX.X, ALU.add).then_inc(normed_in, 1)
                dve.wait_ge(normed_in, n + 1)
                after(dve, log_ready, n - 1)
                nc.vector.tensor_scalar(clipped[:, i % 2, :], norms[:, i % 2, :], 1e-24, None, ALU.max
                                        ).then_inc(clipped_ready, 1)
            n, i = tile_of(it, sigma, 3)
            if n is not None:
                after(dve, values_done, n + 1)
                outs = ps_sim[:, :, 0:4 * (LD + 1)].rearrange("p a (h d) -> p a h d", d=LD + 1)
                nc.vector.reciprocal(inv_sum[:, i % 2, :].rearrange("p (a h d) -> p a h d", a=2, d=1),
                                     outs[:, :, :, LD:]).then_inc(inv_sum_ready, 1)
                dve.wait_ge(inv_sum_ready, n + 1)
                after(dve, heads_turned, n - 1)
                for a in range(2):
                    op = nc.vector.tensor_tensor(
                        heads[:, i % 2, a * 4 * LD:(a + 1) * 4 * LD].rearrange("p (h d) -> p h d", d=LD),
                        outs[:, a, :, 0:LD],
                        inv_sum[:, i % 2, 4 * a:4 * a + 4].rearrange("p (h d) -> p h d", d=1)
                        .broadcast_to((P, 4, LD)), ALU.mult)
                op.then_inc(heads_ready, 1)
            if position(sigma, 2) == VAR:
                late(2)
            late(3)
            if tile_layer is None and 1 <= sigma <= NCH - 2:
                add_gated(dve, sigma - 1)

        @block.vector
        def _(dve):
            nc.vector.memset(v_mix[64:P, 0, :, 0:LD], 0.0).then_inc(cleared, 1)
            nc.vector.memset(k_t[:, 0, :, P:], 0.0).then_inc(cleared, 1)
            nc.vector.memset(norm_bias[:, :], float(0.5 * NORM_SHIFT * np.log(2.0))).then_inc(cleared, 1)
            nc.vector.memset(x_mid[:, 0, 0:1], 0.0)
            nc.vector.memset(v_mix[:, :, :, LD:LD + 1], 1.0).then_inc(cleared, 1)
            nc.vector.memset(v_aug[:, :, :, LD:LD + 1], 1.0).then_inc(cleared, 1)
            iterate(dve, lambda *a: vector_slot(dve, *a))
            for m in range(NCH - 2, NCH):
                add_gated(dve, m)

        def gpsimd_slot(pool, it, sigma, tile_layer, chunk_layer):
            n, i = tile_of(it, sigma, 1)
            if n is not None:
                l = tile_layer if sigma and tile_layer is not None else chunk_layer
                l = 0 if l is None else l
                after(pool, unit_ready, n + 1)
                after(pool, turn_done, n - 1)
                x = unit[:, i % 2, :].rearrange("p (w h d) -> p w h d", w=2, d=LD)
                tab = lambda part: table[:, l, part, i].rearrange("p w (a d) -> p w a d", a=1)
                a_out = turned[:, i % 2, :].rearrange("p (w h d) -> p w h d", w=2, d=LD)
                b_out = turn_sin[:, :].rearrange("p (w h d) -> p w h d", w=2, d=LD)
                for w in range(2):
                    nc.gpsimd.tensor_tensor(a_out[:, w], x[:, w], tab(0)[:, w].broadcast_to((P, LH, LD)), ALU.mult
                                            ).then_inc(rope_step, 1)
                after(pool, rotated, n)
                for half in range(2):
                    d, e = half * LD // 2, (1 - half) * LD // 2
                    for w in range(2):
                        nc.gpsimd.tensor_tensor(b_out[:, w, :, d:d + LD // 2], x[:, w, :, e:e + LD // 2],
                                                tab(1)[:, w, :, d:d + LD // 2].broadcast_to((P, LH, LD // 2)),
                                                ALU.mult).then_inc(rope_step, 1)

        @block.gpsimd
        def _(pool):
            iterate(pool, lambda *a: gpsimd_slot(pool, *a))


def build(nc, dram, out):
    with ExitStack() as whole:
        t = {}

        def sb(name, shape, dt=F32, scope=whole):
            t[name] = scope.enter_context(nc.sbuf_tensor(name, shape, dt))

        sb("identity", [P, P])
        sb("identity_bf", [P, P], BF16)
        sb("center", [P, P])
        sb("mean", [P, P])
        sb("eps_col", [P, 1])
        sb("c_t", [P, B])
        sb("mod", [P, 6, B])
        sb("wo_bv", [P, 1])
        sb("ga_bias", [P, B])
        sb("bias4", [P, 4])
        sb("wo", [D, D])
        sb("x_t", [P, TOK])
        sb("wqkv", [D, DEPTH, 3 * INNER])
        sb("wout", [P, DEPTH, INNER // P, D])
        sb("w1", [D, DEPTH, 2 * HID])
        sb("w2", [P, DEPTH, 3, D])
        sb("b1", [P, DEPTH, 2, 3])
        sb("b2", [P, DEPTH])
        sb("ln_g", [P, DEPTH])
        sb("ln_b", [P, DEPTH])
        sb("table", [P, DEPTH, 2, TPB, 2, LD])
        sb("masks", [P, 2, P], BF16)
        t["part_rows"] = nc.dram_tensor("part_rows", (2, H, len(QROWS), HD, TOK), BF16, kind="Internal").ap()
        t["head_rows"] = nc.dram_tensor("head_rows", (NG, P, TOK), F32, kind="Internal").ap()
        with ExitStack() as first:
            sb("wmod", [D, 6 * D], scope=first)
            sb("wq", [D, D], scope=first)
            sb("wk", [D, D], scope=first)
            sb("wv", [D, D], scope=first)
            sb("v_all", [P, B * TPB, D], scope=first)
            sb("q_stack", [STACK, PAIRS, N], BF16, scope=first)
            sb("k_stack", [STACK, H, N], BF16, scope=first)
            t["low_ready"] = first.enter_context(nc.semaphore("low_ready"))
            t["parts_saved"] = first.enter_context(nc.semaphore("parts_saved"))
            t["stacked"] = [first.enter_context(nc.semaphore(f"stacked{j}")) for j in range(NG)]
            sb("v_slots", [P, NG, TPB, GH, VW], scope=first)
            sb("row_max", [P, 2, TPC, GH], scope=first)
            sb("max_rest", [P, 2, TPC, GH], scope=first)
            sb("zeros", [P, TPC, GH], scope=first)
            sb("max_parts", [P, 2, TPC, GH, MROWS], BF16, scope=first)
            sb("max_rows", [GH * MROWS, 2, CH], BF16, scope=first)
            with ExitStack() as parts:
                sb("qk_parts", [P, 2, 3, TOK], BF16, scope=parts)
                prep_phase(nc, t, dram)
            attention_phase(nc, t, dram)
        with ExitStack() as second:
            sb("xa", [P, B, N + 1], scope=second)
            sb("xb", [P, B, N + 1], scope=second)
            finish_attention_phase(nc, t, dram)
            transformer_phase(nc, t, out)


def shape_constants():
    eye = np.eye(P, dtype=np.float32)
    half = np.arange(0, LD, 2, dtype=np.float32)
    inv_freq = (np.float32(1.0) / np.power(np.float32(10000.0), half / np.float32(LD))).astype(np.float32)
    tok = np.arange(N, dtype=np.float32)
    freqs = np.tile(tok[:, None] * inv_freq[None, :], (1, 2)).astype(np.float64)
    base = ((half + np.float32(0.4 * LD)) / np.float32(1.4 * LD)).astype(np.float64)
    power = ((tok - N // 2) / np.float32(WINDOW // 2)).astype(np.float64)
    scale = np.tile(base[None, :] ** power[:, None], (1, 2))
    sign = np.where(np.arange(LD) < LD // 2, -1.0, 1.0)
    rope = np.empty((N, 2, 2, LD), np.float64)
    for w, s in enumerate((scale, 1.0 / scale)):
        rope[:, 0, w] = np.cos(freqs) * s
        rope[:, 1, w] = np.sin(freqs) * sign * s
    rope = rope.reshape(TPB, P, 2, 2, LD).transpose(1, 2, 0, 3, 4).reshape(P, -1).astype(np.float32)

    masks = np.full((P, 2, P), -1e30, np.float32)
    a, b = np.arange(WINDOW)[:, None], np.arange(WINDOW)[None, :]
    own, before = np.where(b <= a, 0.0, -1e30), np.where(b >= a, 0.0, -1e30)
    for v in range(2):
        masks[:WINDOW, v, :WINDOW] = own
        if v:
            masks[:WINDOW, v, WINDOW:] = before
        masks[WINDOW:, v, :WINDOW] = before
        masks[WINDOW:, v, WINDOW:] = own
    return {"identity": eye, "center": eye - np.float32(1.0 / D),
            "rope": rope, "masks": masks.reshape(P, 2 * P)}


_INS = ["L0_attn_x", "L0_attn_Wq", "L0_attn_bq", "L0_attn_Wk", "L0_attn_bk", "L0_attn_Wv", "L0_attn_bv",
        "L0_attn_Wo", "L0_attn_bo", "L0_ffn_wqkv", "L0_ffn_q_scale", "L0_ffn_k_scale", "L0_ffn_wo", "L0_ffn_ln_g",
        "L0_ffn_ln_b", "L0_ffn_w1", "L0_ffn_b1", "L0_ffn_w2", "L0_ffn_b2", "L0_c", "L0_wmod"]


def kernel(**inputs):
    import concourse.bacc as _bacc
    from concourse.bass_utils import run_bass_kernel_spmd as _run

    nc = _bacc.Bacc("TRN2", target_bir_lowering=False, num_devices=1)
    arrays = {name: np.ascontiguousarray(inputs[name]) for name in _INS}
    arrays.update(shape_constants())
    dram = {name: nc.dram_tensor(f"in_{name}_dram", a.shape, mybir.dt.from_np(a.dtype), kind="ExternalInput").ap()
            for name, a in arrays.items()}
    out = nc.dram_tensor("out_0_dram", (B, N, D), F32, kind="ExternalOutput").ap()
    build(nc, dram, out)
    r = _run(nc, [{f"in_{name}_dram": a for name, a in arrays.items()}], core_ids=[0])
    return r.results[0]["out_0_dram"]
```
